# Optimizing a Trainium2 kernel written in Bass

```python
import numpy as np
import jax
import jax.numpy as jnp

def _softmax(x, axis=-1):
    return jax.nn.softmax(x, axis=axis)
def _gelu(x):
    return jax.nn.gelu(x, approximate=True)
def _silu(x):
    return jax.nn.silu(x)
def _sigmoid(x):
    return jax.nn.sigmoid(x)
def _layernorm(x, axis=-1, eps=1e-5):
    m = jnp.mean(x, axis=axis, keepdims=True)
    v = jnp.var(x, axis=axis, keepdims=True)
    return (x - m) / jnp.sqrt(v + eps)
def _scatter_add(tgt, idx, src, axis=0):
    return tgt.at[idx].add(src)
def _segment_sum(src, seg, n):
    return jax.ops.segment_sum(src, seg, n)

kernel_name = 'mk_conv_preact_d4_conv_nhwc192_a7f274'

def setup_inputs(seed: int = 0):
    np.random.seed(seed)
    _w = jnp.asarray
    def _rec_inputs():
        import jax
        import jax.numpy as jnp
        _gk = jax.random.key(seed)
        x = -0.0005963 + 1.001 * jax.random.normal(jax.random.fold_in(_gk, 1), (4, 64, 64, 192), jnp.float32)
        return x
    x = _rec_inputs()
    def _L0_conv_setup():
        import jax, jax.numpy as jnp
        import numpy as np
        C = 192
        DS = 16
        EXPAND = 2
        DI = EXPAND * C
        DCONV = 4
        DT_RANK = (C + 15) // 16
        B, H, W = (4, 64, 64)

        def silu(x):
            return x * jax.nn.sigmoid(x)

        def mamba_block(xs, in_w, cw, cb, xw, dtw, dtb, Alog, Dv, ow):
            N, L, _ = xs.shape
            xz = jnp.einsum('nlc,dc->nld', xs, in_w)
            u, z = jnp.split(xz, 2, axis=-1)
            u_t = jnp.transpose(u, (0, 2, 1))
            u_pad = jnp.pad(u_t, ((0, 0), (0, 0), (DCONV - 1, 0)))
            uc = jax.lax.conv_general_dilated(u_pad, cw[:, None, :], (1,), 'VALID', feature_group_count=DI)
            uc = silu(uc + cb[None, :, None])
            uc = jnp.transpose(uc, (0, 2, 1))
            x_dbl = jnp.einsum('nld,ed->nle', uc, xw)
            dt, Bp, Cp = jnp.split(x_dbl, [DT_RANK, DT_RANK + DS], axis=-1)
            delta = jax.nn.softplus(jnp.einsum('nlr,dr->nld', dt, dtw) + dtb)
            A = -jnp.exp(Alog)

            def step(h, inp):
                d_t, b_t, c_t, u_t = inp
                dA = jnp.exp(d_t[:, :, None] * A)
                h = dA * h + (d_t * u_t)[:, :, None] * b_t[:, None, :]
                y = jnp.einsum('nds,ns->nd', h, c_t)
                return (h, y)
            h0 = jnp.zeros((N, DI, DS), dtype=xs.dtype)
            ins = (jnp.moveaxis(delta, 1, 0), jnp.moveaxis(Bp, 1, 0), jnp.moveaxis(Cp, 1, 0), jnp.moveaxis(uc, 1, 0))
            _, ys = jax.lax.scan(step, h0, ins)
            y = jnp.moveaxis(ys, 0, 1) + uc * Dv
            y = y * silu(z)
            return jnp.einsum('nld,cd->nlc', y, ow)
        key = jax.random.key(seed)
        ks = jax.random.split(key, 12)
        s = 0.02
        x = jax.random.normal(ks[0], (B, H, W, C), dtype=jnp.float32)
        in_proj_w = jax.random.normal(ks[1], (4, 2 * DI, C), dtype=jnp.float32) * s
        conv_w = jax.random.normal(ks[2], (4, DI, DCONV), dtype=jnp.float32) * 0.2
        conv_b = jnp.zeros((4, DI), dtype=jnp.float32)
        x_proj_w = jax.random.normal(ks[3], (4, DT_RANK + 2 * DS, DI), dtype=jnp.float32) * s
        dt_proj_w = jax.random.normal(ks[4], (4, DI, DT_RANK), dtype=jnp.float32) * 0.1
        dt_proj_b = jax.random.normal(ks[5], (4, DI), dtype=jnp.float32) * 0.1
        A_log = jnp.log(jnp.broadcast_to(jnp.arange(1, DS + 1, dtype=jnp.float32), (4, DI, DS)))
        D_skip = jnp.ones((4, DI), dtype=jnp.float32)
        out_proj_w = jax.random.normal(ks[6], (4, C, DI), dtype=jnp.float32) * s
        fc_w = jax.random.normal(ks[7], (C, 4 * C), dtype=jnp.float32) * s
        fc_b = jnp.zeros((C,), dtype=jnp.float32)
        return {'x': x, 'in_proj_w': in_proj_w, 'conv_w': conv_w, 'conv_b': conv_b, 'x_proj_w': x_proj_w, 'dt_proj_w': dt_proj_w, 'dt_proj_b': dt_proj_b, 'A_log': A_log, 'D_skip': D_skip, 'out_proj_w': out_proj_w, 'fc_w': fc_w, 'fc_b': fc_b}
    _L0_conv_all = _L0_conv_setup()
    _L0_conv_in = {k: v for k, v in _L0_conv_all.items() if k in ('in_proj_w', 'conv_w', 'conv_b', 'x_proj_w', 'dt_proj_w', 'dt_proj_b', 'A_log', 'D_skip', 'out_proj_w', 'fc_w', 'fc_b', )}
    del _L0_conv_all

    def _L1_conv_setup():
        import jax, jax.numpy as jnp
        import numpy as np
        B, H, W, DM = (2, 64, 64, 192)
        DI, DS, DR, DC = (384, 16, 12, 3)

        def hscan1(t):
            odd = (jnp.arange(t.shape[2]) % 2 == 1)[:, None]
            return jnp.where(odd, t[..., ::-1], t)

        def selective_scan(u, delta, A, Bm, Cm, D):
            dA = jnp.exp(delta[..., None] * A[None, :, None, :])
            dBu = (delta * u)[..., None] * Bm[:, None, :, :]

            def comb(c1, c2):
                a1, b1 = c1
                a2, b2 = c2
                return (a2 * a1, a2 * b1 + b2)
            _, h = jax.lax.associative_scan(comb, (dA, dBu), axis=2)
            y = jnp.einsum('bdln,bln->bdl', h, Cm)
            return y + u * D[None, :, None]
        key = jax.random.key(seed)
        ks = jax.random.split(key, 8)
        return {'x': jax.random.normal(ks[0], (B, H, W, DM), jnp.float32), 'in_proj_w': jax.random.normal(ks[1], (2 * DI, DM), jnp.float32) * 0.02, 'conv_w': jax.random.normal(ks[2], (DI, 1, DC, DC), jnp.float32) * 0.1, 'conv_b': jnp.zeros((DI,), jnp.float32), 'x_proj_w': jax.random.normal(ks[3], (DR + 2 * DS, DI), jnp.float32) * 0.02, 'dt_w': jax.random.uniform(ks[4], (DI, DR), jnp.float32, -DR ** (-0.5), DR ** (-0.5)), 'dt_b': jax.random.normal(ks[5], (DI,), jnp.float32) * 0.1, 'A_logs': jnp.log(jnp.broadcast_to(jnp.arange(1, DS + 1, dtype=jnp.float32), (DI, DS))), 'Ds': jnp.ones((DI,), jnp.float32), 'ln_w': jnp.ones((DI,), jnp.float32), 'ln_b': jnp.zeros((DI,), jnp.float32), 'out_proj_w': jax.random.normal(ks[6], (DM, DI), jnp.float32) * 0.02}
    _L1_conv_all = _L1_conv_setup()
    _L1_conv_in = {k: v for k, v in _L1_conv_all.items() if k in ('in_proj_w', 'conv_w', 'conv_b', 'x_proj_w', 'dt_w', 'dt_b', 'A_logs', 'Ds', 'ln_w', 'ln_b', 'out_proj_w', )}
    del _L1_conv_all

    def _L2_conv_setup():
        import math
        import jax, jax.numpy as jnp
        import numpy as np
        C_DIM, N_STATE, K_DIR = (192, 16, 4)
        D_RANK = math.ceil(C_DIM / 16)
        B_SZ, H_SZ, W_SZ = (2, 64, 64)

        def _ss2d(x, in_proj_w, conv_w, conv_b, x_proj_w, dt_w, dt_b, A_logs, Ds, ln_g, ln_b, out_w):
            B, H, W, C = x.shape
            L = H * W
            dr = dt_w.shape[1]
            N = A_logs.shape[-1]
            K = A_logs.shape[0]
            xz = x @ in_proj_w
            x_ssm, z = (xz[..., :C], xz[..., C:])
            xc = jnp.transpose(x_ssm, (0, 3, 1, 2))
            xc = jax.lax.conv_general_dilated(xc, conv_w, (1, 1), 'SAME', feature_group_count=C)
            xc = jax.nn.silu(xc + conv_b[None, :, None, None])
            x0 = xc.reshape(B, C, L)
            x1 = x0[..., ::-1]
            x2 = jnp.transpose(xc, (0, 1, 3, 2)).reshape(B, C, L)
            x3 = x2[..., ::-1]
            xs = jnp.stack([x0, x1, x2, x3], axis=0)
            proj = jnp.einsum('kbcl,kcd->kbld', xs, x_proj_w)
            dpart = proj[..., :dr]
            Bm = proj[..., dr:dr + N]
            Cm = proj[..., dr + N:]
            delta = jnp.einsum('kblr,krc->kblc', dpart, dt_w) + dt_b[:, None, None, :]
            delta = jax.nn.softplus(delta + dt_b[:, None, None, :])
            A_neg = -jnp.exp(A_logs)
            u_t = jnp.transpose(xs, (3, 0, 1, 2))
            d_t = jnp.transpose(delta, (2, 0, 1, 3))
            B_t = jnp.transpose(Bm, (2, 0, 1, 3))
            C_t = jnp.transpose(Cm, (2, 0, 1, 3))

            def step(state, inp):
                d, b, c, uu = inp
                dA = jnp.exp(d[..., None] * A_neg[:, None, :, :])
                state = dA * state + (d * uu)[..., None] * b[:, :, None, :]
                y = jnp.einsum('kbcn,kbn->kbc', state, c)
                return (state, y)
            init = jnp.zeros((K, B, C, N), jnp.float32)
            _, ys = jax.lax.scan(step, init, (d_t, B_t, C_t, u_t))
            ys = jnp.transpose(ys, (1, 2, 3, 0))
            ys = ys + Ds[:, None, :, None] * xs
            y0 = ys[0].reshape(B, C, H, W)
            y1 = ys[1][..., ::-1].reshape(B, C, H, W)
            y2 = jnp.transpose(ys[2].reshape(B, C, W, H), (0, 1, 3, 2))
            y3 = jnp.transpose(ys[3][..., ::-1].reshape(B, C, W, H), (0, 1, 3, 2))
            y = y0 + y1 + y2 + y3
            y = jnp.transpose(y, (0, 2, 3, 1))
            mu = y.mean(-1, keepdims=True)
            var = y.var(-1, keepdims=True)
            y = (y - mu) / jnp.sqrt(var + 1e-05) * ln_g + ln_b
            y = y * jax.nn.silu(z)
            return y @ out_w
        key = jax.random.key(seed)
        ks = jax.random.split(key, 8)
        C, N, K, dr = (C_DIM, N_STATE, K_DIR, D_RANK)
        x = jax.random.normal(ks[0], (B_SZ, H_SZ, W_SZ, C), jnp.float32)
        in_proj_w = jax.random.normal(ks[1], (C, 2 * C), jnp.float32) / math.sqrt(C)
        conv_w = jax.random.normal(ks[2], (C, 1, 3, 3), jnp.float32) * 0.1
        conv_b = jnp.zeros((C,), jnp.float32)
        x_proj_w = jax.random.normal(ks[3], (K, C, dr + 2 * N), jnp.float32) / math.sqrt(C)
        dt_w = jax.random.normal(ks[4], (K, dr, C), jnp.float32) / math.sqrt(dr)
        dt_min, dt_max, floor = (0.001, 0.1, 0.0001)
        r = jax.random.uniform(ks[5], (K, C), jnp.float32)
        dt_init = jnp.clip(jnp.exp(r * (math.log(dt_max) - math.log(dt_min)) + math.log(dt_min)), floor, None)
        dt_b = dt_init + jnp.log(-jnp.expm1(-dt_init))
        A_logs = jnp.tile(jnp.log(jnp.arange(1, N + 1, dtype=jnp.float32))[None, None, :], (K, C, 1))
        Ds = jnp.ones((K, C), jnp.float32)
        ln_g = jnp.ones((C,), jnp.float32)
        ln_b = jnp.zeros((C,), jnp.float32)
        out_w = jax.random.normal(ks[6], (C, C), jnp.float32) / math.sqrt(C)
        return dict(x=x, in_proj_w=in_proj_w, conv_w=conv_w, conv_b=conv_b, x_proj_w=x_proj_w, dt_w=dt_w, dt_b=dt_b, A_logs=A_logs, Ds=Ds, ln_g=ln_g, ln_b=ln_b, out_w=out_w)
    _L2_conv_all = _L2_conv_setup()
    _L2_conv_in = {k: v for k, v in _L2_conv_all.items() if k in ('in_proj_w', 'conv_w', 'conv_b', 'x_proj_w', 'dt_w', 'dt_b', 'A_logs', 'Ds', 'ln_g', 'ln_b', 'out_w', )}
    del _L2_conv_all

    def _L3_conv_setup():
        import jax, jax.numpy as jnp
        import numpy as np
        D_MODEL = 192
        D_STATE = 16
        D_CONV = 3
        EXPAND = 2
        D_INNER = EXPAND * D_MODEL
        DT_RANK = (D_MODEL + 15) // 16
        K = 4
        B, H, W = (2, 64, 64)
        EPS = 1e-05

        def silu(x):
            return x * jax.nn.sigmoid(x)

        def _ss2d_forward(x, in_proj_w, conv_w, conv_b, x_proj_weight, dt_projs_weight, dt_projs_bias, A_logs, Ds, ln_gamma, ln_beta, out_proj_w):
            b, h, w, _ = x.shape
            L = h * w
            xz = jnp.einsum('bhwc,dc->bhwd', x, in_proj_w)
            xc, z = jnp.split(xz, 2, axis=-1)
            xc = jnp.transpose(xc, (0, 3, 1, 2))
            xc = jax.lax.conv_general_dilated(xc, conv_w, window_strides=(1, 1), padding=((1, 1), (1, 1)), feature_group_count=D_INNER, dimension_numbers=('NCHW', 'OIHW', 'NCHW'))
            xc = silu(xc + conv_b[None, :, None, None])
            x_flat = xc.reshape(b, D_INNER, L)
            x_t = jnp.transpose(xc, (0, 1, 3, 2)).reshape(b, D_INNER, L)
            xs = jnp.stack([x_flat, x_t], axis=1)
            xs = jnp.concatenate([xs, jnp.flip(xs, axis=-1)], axis=1)
            x_dbl = jnp.einsum('bkdl,kcd->bkcl', xs, x_proj_weight)
            dts = x_dbl[:, :, :DT_RANK]
            Bmat = x_dbl[:, :, DT_RANK:DT_RANK + D_STATE]
            Cmat = x_dbl[:, :, DT_RANK + D_STATE:]
            dts = jnp.einsum('bkrl,kdr->bkdl', dts, dt_projs_weight)
            delta = jax.nn.softplus(dts + dt_projs_bias[None, :, :, None])
            A = -jnp.exp(A_logs).reshape(K, D_INNER, D_STATE)
            u_t = jnp.transpose(xs, (3, 0, 1, 2))
            d_t = jnp.transpose(delta, (3, 0, 1, 2))
            B_t = jnp.transpose(Bmat, (3, 0, 1, 2))
            C_t = jnp.transpose(Cmat, (3, 0, 1, 2))

            def step(hst, inp):
                d, bm, cm, uu = inp
                dA = jnp.exp(d[..., None] * A[None])
                dBu = (d * uu)[..., None] * bm[:, :, None, :]
                hst = dA * hst + dBu
                y = jnp.einsum('bkdn,bkn->bkd', hst, cm)
                return (hst, y)
            h0 = jnp.zeros((b, K, D_INNER, D_STATE), dtype=x.dtype)
            _, ys = jax.lax.scan(step, h0, (d_t, B_t, C_t, u_t))
            ys = jnp.transpose(ys, (1, 2, 3, 0))
            ys = ys + xs * Ds.reshape(K, D_INNER)[None, :, :, None]
            y1 = ys[:, 0]
            inv2 = jnp.flip(ys[:, 2], axis=-1)
            wh = jnp.transpose(ys[:, 1].reshape(b, D_INNER, w, h), (0, 1, 3, 2)).reshape(b, D_INNER, L)
            invwh = jnp.transpose(jnp.flip(ys[:, 3], axis=-1).reshape(b, D_INNER, w, h), (0, 1, 3, 2)).reshape(b, D_INNER, L)
            y = y1 + inv2 + wh + invwh
            y = jnp.transpose(y, (0, 2, 1)).reshape(b, h, w, D_INNER)
            mu = jnp.mean(y, axis=-1, keepdims=True)
            var = jnp.var(y, axis=-1, keepdims=True)
            y = (y - mu) * jax.lax.rsqrt(var + EPS) * ln_gamma + ln_beta
            y = y * silu(z)
            return jnp.einsum('bhwd,cd->bhwc', y, out_proj_w)
        key = jax.random.key(seed)
        ks = jax.random.split(key, 12)
        s = 0.02
        x = jax.random.normal(ks[0], (B, H, W, D_MODEL), dtype=jnp.float32)
        in_proj_w = jax.random.normal(ks[1], (2 * D_INNER, D_MODEL), dtype=jnp.float32) * s
        conv_w = jax.random.normal(ks[2], (D_INNER, 1, D_CONV, D_CONV), dtype=jnp.float32) * 0.1
        conv_b = jnp.zeros((D_INNER,), dtype=jnp.float32)
        x_proj_weight = jax.random.normal(ks[3], (K, DT_RANK + 2 * D_STATE, D_INNER), dtype=jnp.float32) * s
        dt_projs_weight = jax.random.normal(ks[4], (K, D_INNER, DT_RANK), dtype=jnp.float32) * DT_RANK ** (-0.5)
        dt_projs_bias = jax.random.uniform(ks[5], (K, D_INNER), dtype=jnp.float32, minval=-4.0, maxval=-2.0)
        A_logs = jnp.log(jnp.tile(jnp.arange(1, D_STATE + 1, dtype=jnp.float32), (K * D_INNER, 1)))
        Ds = jnp.ones((K * D_INNER,), dtype=jnp.float32)
        ln_gamma = jnp.ones((D_INNER,), dtype=jnp.float32)
        ln_beta = jnp.zeros((D_INNER,), dtype=jnp.float32)
        out_proj_w = jax.random.normal(ks[6], (D_MODEL, D_INNER), dtype=jnp.float32) * s
        return dict(x=x, in_proj_w=in_proj_w, conv_w=conv_w, conv_b=conv_b, x_proj_weight=x_proj_weight, dt_projs_weight=dt_projs_weight, dt_projs_bias=dt_projs_bias, A_logs=A_logs, Ds=Ds, ln_gamma=ln_gamma, ln_beta=ln_beta, out_proj_w=out_proj_w)
    _L3_conv_all = _L3_conv_setup()
    _L3_conv_in = {k: v for k, v in _L3_conv_all.items() if k in ('in_proj_w', 'conv_w', 'conv_b', 'x_proj_weight', 'dt_projs_weight', 'dt_projs_bias', 'A_logs', 'Ds', 'ln_gamma', 'ln_beta', 'out_proj_w', )}
    del _L3_conv_all

    return {
        "x": x,
        "L0_conv_in_proj_w": _L0_conv_in["in_proj_w"],
        "L0_conv_conv_w": _L0_conv_in["conv_w"],
        "L0_conv_conv_b": _L0_conv_in["conv_b"],
        "L0_conv_x_proj_w": _L0_conv_in["x_proj_w"],
        "L0_conv_dt_proj_w": _L0_conv_in["dt_proj_w"],
        "L0_conv_dt_proj_b": _L0_conv_in["dt_proj_b"],
        "L0_conv_A_log": _L0_conv_in["A_log"],
        "L0_conv_D_skip": _L0_conv_in["D_skip"],
        "L0_conv_out_proj_w": _L0_conv_in["out_proj_w"],
        "L0_conv_fc_w": _L0_conv_in["fc_w"],
        "L0_conv_fc_b": _L0_conv_in["fc_b"],
        "L1_conv_in_proj_w": _L1_conv_in["in_proj_w"],
        "L1_conv_conv_w": _L1_conv_in["conv_w"],
        "L1_conv_conv_b": _L1_conv_in["conv_b"],
        "L1_conv_x_proj_w": _L1_conv_in["x_proj_w"],
        "L1_conv_dt_w": _L1_conv_in["dt_w"],
        "L1_conv_dt_b": _L1_conv_in["dt_b"],
        "L1_conv_A_logs": _L1_conv_in["A_logs"],
        "L1_conv_Ds": _L1_conv_in["Ds"],
        "L1_conv_ln_w": _L1_conv_in["ln_w"],
        "L1_conv_ln_b": _L1_conv_in["ln_b"],
        "L1_conv_out_proj_w": _L1_conv_in["out_proj_w"],
        "L2_conv_in_proj_w": _L2_conv_in["in_proj_w"],
        "L2_conv_conv_w": _L2_conv_in["conv_w"],
        "L2_conv_conv_b": _L2_conv_in["conv_b"],
        "L2_conv_x_proj_w": _L2_conv_in["x_proj_w"],
        "L2_conv_dt_w": _L2_conv_in["dt_w"],
        "L2_conv_dt_b": _L2_conv_in["dt_b"],
        "L2_conv_A_logs": _L2_conv_in["A_logs"],
        "L2_conv_Ds": _L2_conv_in["Ds"],
        "L2_conv_ln_g": _L2_conv_in["ln_g"],
        "L2_conv_ln_b": _L2_conv_in["ln_b"],
        "L2_conv_out_w": _L2_conv_in["out_w"],
        "L3_conv_in_proj_w": _L3_conv_in["in_proj_w"],
        "L3_conv_conv_w": _L3_conv_in["conv_w"],
        "L3_conv_conv_b": _L3_conv_in["conv_b"],
        "L3_conv_x_proj_weight": _L3_conv_in["x_proj_weight"],
        "L3_conv_dt_projs_weight": _L3_conv_in["dt_projs_weight"],
        "L3_conv_dt_projs_bias": _L3_conv_in["dt_projs_bias"],
        "L3_conv_A_logs": _L3_conv_in["A_logs"],
        "L3_conv_Ds": _L3_conv_in["Ds"],
        "L3_conv_ln_gamma": _L3_conv_in["ln_gamma"],
        "L3_conv_ln_beta": _L3_conv_in["ln_beta"],
        "L3_conv_out_proj_w": _L3_conv_in["out_proj_w"],
    }

def reference(x, L0_conv_in_proj_w, L0_conv_conv_w, L0_conv_conv_b, L0_conv_x_proj_w, L0_conv_dt_proj_w, L0_conv_dt_proj_b, L0_conv_A_log, L0_conv_D_skip, L0_conv_out_proj_w, L0_conv_fc_w, L0_conv_fc_b, L1_conv_in_proj_w, L1_conv_conv_w, L1_conv_conv_b, L1_conv_x_proj_w, L1_conv_dt_w, L1_conv_dt_b, L1_conv_A_logs, L1_conv_Ds, L1_conv_ln_w, L1_conv_ln_b, L1_conv_out_proj_w, L2_conv_in_proj_w, L2_conv_conv_w, L2_conv_conv_b, L2_conv_x_proj_w, L2_conv_dt_w, L2_conv_dt_b, L2_conv_A_logs, L2_conv_Ds, L2_conv_ln_g, L2_conv_ln_b, L2_conv_out_w, L3_conv_in_proj_w, L3_conv_conv_w, L3_conv_conv_b, L3_conv_x_proj_weight, L3_conv_dt_projs_weight, L3_conv_dt_projs_bias, L3_conv_A_logs, L3_conv_Ds, L3_conv_ln_gamma, L3_conv_ln_beta, L3_conv_out_proj_w):
    import jax
    import jax.numpy as jnp
    def _L0_conv_ref(x, in_proj_w, conv_w, conv_b, x_proj_w, dt_proj_w, dt_proj_b, A_log, D_skip, out_proj_w, fc_w, fc_b):
        import jax, jax.numpy as jnp
        import numpy as np
        C = 192
        DS = 16
        EXPAND = 2
        DI = EXPAND * C
        DCONV = 4
        DT_RANK = (C + 15) // 16
        B, H, W = (4, 64, 64)

        def silu(x):
            return x * jax.nn.sigmoid(x)

        def mamba_block(xs, in_w, cw, cb, xw, dtw, dtb, Alog, Dv, ow):
            N, L, _ = xs.shape
            xz = jnp.einsum('nlc,dc->nld', xs, in_w)
            u, z = jnp.split(xz, 2, axis=-1)
            u_t = jnp.transpose(u, (0, 2, 1))
            u_pad = jnp.pad(u_t, ((0, 0), (0, 0), (DCONV - 1, 0)))
            uc = jax.lax.conv_general_dilated(u_pad, cw[:, None, :], (1,), 'VALID', feature_group_count=DI)
            uc = silu(uc + cb[None, :, None])
            uc = jnp.transpose(uc, (0, 2, 1))
            x_dbl = jnp.einsum('nld,ed->nle', uc, xw)
            dt, Bp, Cp = jnp.split(x_dbl, [DT_RANK, DT_RANK + DS], axis=-1)
            delta = jax.nn.softplus(jnp.einsum('nlr,dr->nld', dt, dtw) + dtb)
            A = -jnp.exp(Alog)

            def step(h, inp):
                d_t, b_t, c_t, u_t = inp
                dA = jnp.exp(d_t[:, :, None] * A)
                h = dA * h + (d_t * u_t)[:, :, None] * b_t[:, None, :]
                y = jnp.einsum('nds,ns->nd', h, c_t)
                return (h, y)
            h0 = jnp.zeros((N, DI, DS), dtype=xs.dtype)
            ins = (jnp.moveaxis(delta, 1, 0), jnp.moveaxis(Bp, 1, 0), jnp.moveaxis(Cp, 1, 0), jnp.moveaxis(uc, 1, 0))
            _, ys = jax.lax.scan(step, h0, ins)
            y = jnp.moveaxis(ys, 0, 1) + uc * Dv
            y = y * silu(z)
            return jnp.einsum('nld,cd->nlc', y, ow)
        Bb, Hh, Ww, Cc = x.shape

        def m(i, seq):
            return mamba_block(seq, in_proj_w[i], conv_w[i], conv_b[i], x_proj_w[i], dt_proj_w[i], dt_proj_b[i], A_log[i], D_skip[i], out_proj_w[i])
        x_h = x.reshape(-1, Ww, Cc)
        h1 = m(0, x_h)
        h2 = jnp.flip(m(1, jnp.flip(x_h, axis=1)), axis=1)
        h = jnp.concatenate([h1, h2], axis=-1).reshape(Bb, Hh, Ww, -1)
        x_v = jnp.transpose(x, (0, 2, 1, 3)).reshape(-1, Hh, Cc)
        v1 = m(2, x_v)
        v2 = jnp.flip(m(3, jnp.flip(x_v, axis=1)), axis=1)
        v = jnp.concatenate([v1, v2], axis=-1).reshape(Bb, Ww, Hh, -1)
        v = jnp.transpose(v, (0, 2, 1, 3))
        out = jnp.concatenate([v, h], axis=-1)
        return jnp.einsum('bhwd,cd->bhwc', out, fc_w) + fc_b

    def _L1_conv_ref(x, in_proj_w, conv_w, conv_b, x_proj_w, dt_w, dt_b, A_logs, Ds, ln_w, ln_b, out_proj_w):
        import jax, jax.numpy as jnp
        import numpy as np
        B, H, W, DM = (2, 64, 64, 192)
        DI, DS, DR, DC = (384, 16, 12, 3)

        def hscan1(t):
            odd = (jnp.arange(t.shape[2]) % 2 == 1)[:, None]
            return jnp.where(odd, t[..., ::-1], t)

        def selective_scan(u, delta, A, Bm, Cm, D):
            dA = jnp.exp(delta[..., None] * A[None, :, None, :])
            dBu = (delta * u)[..., None] * Bm[:, None, :, :]

            def comb(c1, c2):
                a1, b1 = c1
                a2, b2 = c2
                return (a2 * a1, a2 * b1 + b2)
            _, h = jax.lax.associative_scan(comb, (dA, dBu), axis=2)
            y = jnp.einsum('bdln,bln->bdl', h, Cm)
            return y + u * D[None, :, None]
        Bb, Hh, Ww, _ = x.shape
        L = Hh * Ww
        xz = x @ in_proj_w.T
        xc, z = jnp.split(xz, 2, axis=-1)
        xc = xc.transpose(0, 3, 1, 2)
        xc = jax.lax.conv_general_dilated(xc, conv_w, (1, 1), 'SAME', feature_group_count=xc.shape[1])
        xc = jax.nn.silu(xc + conv_b[None, :, None, None])
        xs = hscan1(xc).reshape(Bb, -1, L)
        x_dbl = jnp.einsum('bdl,cd->bcl', xs, x_proj_w)
        dts, Bs, Cs = jnp.split(x_dbl, [DR, DR + DS], axis=1)
        dts = jnp.einsum('brl,dr->bdl', dts, dt_w)
        delta = jax.nn.softplus(dts + dt_b[None, :, None])
        A = -jnp.exp(A_logs)
        y = selective_scan(xs, delta, A, Bs.transpose(0, 2, 1), Cs.transpose(0, 2, 1), Ds)
        y = hscan1(y.reshape(Bb, -1, Hh, Ww))
        y = y.transpose(0, 2, 3, 1)
        mu = y.mean(-1, keepdims=True)
        var = y.var(-1, keepdims=True)
        y = (y - mu) / jnp.sqrt(var + 1e-05) * ln_w + ln_b
        y = y * jax.nn.silu(z)
        return y @ out_proj_w.T

    def _L2_conv_ref(x, in_proj_w, conv_w, conv_b, x_proj_w, dt_w, dt_b, A_logs, Ds, ln_g, ln_b, out_w):
        import math
        import jax, jax.numpy as jnp
        import numpy as np
        C_DIM, N_STATE, K_DIR = (192, 16, 4)
        D_RANK = math.ceil(C_DIM / 16)
        B_SZ, H_SZ, W_SZ = (2, 64, 64)

        def _ss2d(x, in_proj_w, conv_w, conv_b, x_proj_w, dt_w, dt_b, A_logs, Ds, ln_g, ln_b, out_w):
            B, H, W, C = x.shape
            L = H * W
            dr = dt_w.shape[1]
            N = A_logs.shape[-1]
            K = A_logs.shape[0]
            xz = x @ in_proj_w
            x_ssm, z = (xz[..., :C], xz[..., C:])
            xc = jnp.transpose(x_ssm, (0, 3, 1, 2))
            xc = jax.lax.conv_general_dilated(xc, conv_w, (1, 1), 'SAME', feature_group_count=C)
            xc = jax.nn.silu(xc + conv_b[None, :, None, None])
            x0 = xc.reshape(B, C, L)
            x1 = x0[..., ::-1]
            x2 = jnp.transpose(xc, (0, 1, 3, 2)).reshape(B, C, L)
            x3 = x2[..., ::-1]
            xs = jnp.stack([x0, x1, x2, x3], axis=0)
            proj = jnp.einsum('kbcl,kcd->kbld', xs, x_proj_w)
            dpart = proj[..., :dr]
            Bm = proj[..., dr:dr + N]
            Cm = proj[..., dr + N:]
            delta = jnp.einsum('kblr,krc->kblc', dpart, dt_w) + dt_b[:, None, None, :]
            delta = jax.nn.softplus(delta + dt_b[:, None, None, :])
            A_neg = -jnp.exp(A_logs)
            u_t = jnp.transpose(xs, (3, 0, 1, 2))
            d_t = jnp.transpose(delta, (2, 0, 1, 3))
            B_t = jnp.transpose(Bm, (2, 0, 1, 3))
            C_t = jnp.transpose(Cm, (2, 0, 1, 3))

            def step(state, inp):
                d, b, c, uu = inp
                dA = jnp.exp(d[..., None] * A_neg[:, None, :, :])
                state = dA * state + (d * uu)[..., None] * b[:, :, None, :]
                y = jnp.einsum('kbcn,kbn->kbc', state, c)
                return (state, y)
            init = jnp.zeros((K, B, C, N), jnp.float32)
            _, ys = jax.lax.scan(step, init, (d_t, B_t, C_t, u_t))
            ys = jnp.transpose(ys, (1, 2, 3, 0))
            ys = ys + Ds[:, None, :, None] * xs
            y0 = ys[0].reshape(B, C, H, W)
            y1 = ys[1][..., ::-1].reshape(B, C, H, W)
            y2 = jnp.transpose(ys[2].reshape(B, C, W, H), (0, 1, 3, 2))
            y3 = jnp.transpose(ys[3][..., ::-1].reshape(B, C, W, H), (0, 1, 3, 2))
            y = y0 + y1 + y2 + y3
            y = jnp.transpose(y, (0, 2, 3, 1))
            mu = y.mean(-1, keepdims=True)
            var = y.var(-1, keepdims=True)
            y = (y - mu) / jnp.sqrt(var + 1e-05) * ln_g + ln_b
            y = y * jax.nn.silu(z)
            return y @ out_w
        return _ss2d(x, in_proj_w, conv_w, conv_b, x_proj_w, dt_w, dt_b, A_logs, Ds, ln_g, ln_b, out_w)

    def _L3_conv_ref(x, in_proj_w, conv_w, conv_b, x_proj_weight, dt_projs_weight, dt_projs_bias, A_logs, Ds, ln_gamma, ln_beta, out_proj_w):
        import jax, jax.numpy as jnp
        import numpy as np
        D_MODEL = 192
        D_STATE = 16
        D_CONV = 3
        EXPAND = 2
        D_INNER = EXPAND * D_MODEL
        DT_RANK = (D_MODEL + 15) // 16
        K = 4
        B, H, W = (2, 64, 64)
        EPS = 1e-05

        def silu(x):
            return x * jax.nn.sigmoid(x)

        def _ss2d_forward(x, in_proj_w, conv_w, conv_b, x_proj_weight, dt_projs_weight, dt_projs_bias, A_logs, Ds, ln_gamma, ln_beta, out_proj_w):
            b, h, w, _ = x.shape
            L = h * w
            xz = jnp.einsum('bhwc,dc->bhwd', x, in_proj_w)
            xc, z = jnp.split(xz, 2, axis=-1)
            xc = jnp.transpose(xc, (0, 3, 1, 2))
            xc = jax.lax.conv_general_dilated(xc, conv_w, window_strides=(1, 1), padding=((1, 1), (1, 1)), feature_group_count=D_INNER, dimension_numbers=('NCHW', 'OIHW', 'NCHW'))
            xc = silu(xc + conv_b[None, :, None, None])
            x_flat = xc.reshape(b, D_INNER, L)
            x_t = jnp.transpose(xc, (0, 1, 3, 2)).reshape(b, D_INNER, L)
            xs = jnp.stack([x_flat, x_t], axis=1)
            xs = jnp.concatenate([xs, jnp.flip(xs, axis=-1)], axis=1)
            x_dbl = jnp.einsum('bkdl,kcd->bkcl', xs, x_proj_weight)
            dts = x_dbl[:, :, :DT_RANK]
            Bmat = x_dbl[:, :, DT_RANK:DT_RANK + D_STATE]
            Cmat = x_dbl[:, :, DT_RANK + D_STATE:]
            dts = jnp.einsum('bkrl,kdr->bkdl', dts, dt_projs_weight)
            delta = jax.nn.softplus(dts + dt_projs_bias[None, :, :, None])
            A = -jnp.exp(A_logs).reshape(K, D_INNER, D_STATE)
            u_t = jnp.transpose(xs, (3, 0, 1, 2))
            d_t = jnp.transpose(delta, (3, 0, 1, 2))
            B_t = jnp.transpose(Bmat, (3, 0, 1, 2))
            C_t = jnp.transpose(Cmat, (3, 0, 1, 2))

            def step(hst, inp):
                d, bm, cm, uu = inp
                dA = jnp.exp(d[..., None] * A[None])
                dBu = (d * uu)[..., None] * bm[:, :, None, :]
                hst = dA * hst + dBu
                y = jnp.einsum('bkdn,bkn->bkd', hst, cm)
                return (hst, y)
            h0 = jnp.zeros((b, K, D_INNER, D_STATE), dtype=x.dtype)
            _, ys = jax.lax.scan(step, h0, (d_t, B_t, C_t, u_t))
            ys = jnp.transpose(ys, (1, 2, 3, 0))
            ys = ys + xs * Ds.reshape(K, D_INNER)[None, :, :, None]
            y1 = ys[:, 0]
            inv2 = jnp.flip(ys[:, 2], axis=-1)
            wh = jnp.transpose(ys[:, 1].reshape(b, D_INNER, w, h), (0, 1, 3, 2)).reshape(b, D_INNER, L)
            invwh = jnp.transpose(jnp.flip(ys[:, 3], axis=-1).reshape(b, D_INNER, w, h), (0, 1, 3, 2)).reshape(b, D_INNER, L)
            y = y1 + inv2 + wh + invwh
            y = jnp.transpose(y, (0, 2, 1)).reshape(b, h, w, D_INNER)
            mu = jnp.mean(y, axis=-1, keepdims=True)
            var = jnp.var(y, axis=-1, keepdims=True)
            y = (y - mu) * jax.lax.rsqrt(var + EPS) * ln_gamma + ln_beta
            y = y * silu(z)
            return jnp.einsum('bhwd,cd->bhwc', y, out_proj_w)
        return _ss2d_forward(x, in_proj_w, conv_w, conv_b, x_proj_weight, dt_projs_weight, dt_projs_bias, A_logs, Ds, ln_gamma, ln_beta, out_proj_w)

    def _gn(v, G=32, eps=1e-5):
        B_, H_, W_, C_ = v.shape
        g = v.reshape(B_, H_, W_, G, C_ // G)
        m = jnp.mean(g, axis=(1, 2, 4), keepdims=True)
        s = jnp.var(g, axis=(1, 2, 4), keepdims=True)
        return ((g - m) / jnp.sqrt(s + eps)).reshape(v.shape)

    def _ln_c(v, eps=1e-6):
        m = jnp.mean(v, axis=-1, keepdims=True)
        s = jnp.var(v, axis=-1, keepdims=True)
        return (v - m) / jnp.sqrt(s + eps)

    def _ln_t(v, eps=1e-5):
        m = jnp.mean(v, axis=-1, keepdims=True)
        s = jnp.var(v, axis=-1, keepdims=True)
        return (v - m) / jnp.sqrt(s + eps)

    def _to_tokens(v):
        B_, H_, W_, C_ = v.shape
        return v.reshape(B_, H_ * W_, C_)
    def _from_tokens(t, like):
        return t.reshape(like.shape)

    x = x + _L0_conv_ref(_gn(x), L0_conv_in_proj_w, L0_conv_conv_w, L0_conv_conv_b, L0_conv_x_proj_w, L0_conv_dt_proj_w, L0_conv_dt_proj_b, L0_conv_A_log, L0_conv_D_skip, L0_conv_out_proj_w, L0_conv_fc_w, L0_conv_fc_b)
    x = x + _L1_conv_ref(_gn(x), L1_conv_in_proj_w, L1_conv_conv_w, L1_conv_conv_b, L1_conv_x_proj_w, L1_conv_dt_w, L1_conv_dt_b, L1_conv_A_logs, L1_conv_Ds, L1_conv_ln_w, L1_conv_ln_b, L1_conv_out_proj_w)
    x = x + _L2_conv_ref(_gn(x), L2_conv_in_proj_w, L2_conv_conv_w, L2_conv_conv_b, L2_conv_x_proj_w, L2_conv_dt_w, L2_conv_dt_b, L2_conv_A_logs, L2_conv_Ds, L2_conv_ln_g, L2_conv_ln_b, L2_conv_out_w)
    x = x + _L3_conv_ref(_gn(x), L3_conv_in_proj_w, L3_conv_conv_w, L3_conv_conv_b, L3_conv_x_proj_weight, L3_conv_dt_projs_weight, L3_conv_dt_projs_bias, L3_conv_A_logs, L3_conv_Ds, L3_conv_ln_gamma, L3_conv_ln_beta, L3_conv_out_proj_w)
    return x


_drawn_inputs = setup_inputs


def setup_inputs(seed=0):
    import zlib

    import numpy as np

    out = dict(_drawn_inputs(seed))
    spreads = {'L0_conv_conv_b': (0.0, 0.1),
     'L0_conv_D_skip': (1.0, 0.2),
     'L0_conv_fc_b': (0.0, 0.1),
     'L1_conv_conv_b': (0.0, 0.1),
     'L1_conv_Ds': (1.0, 0.2),
     'L1_conv_ln_w': (1.0, 0.2),
     'L1_conv_ln_b': (0.0, 0.1),
     'L2_conv_conv_b': (0.0, 0.1),
     'L2_conv_Ds': (1.0, 0.2),
     'L2_conv_ln_g': (1.0, 0.2),
     'L2_conv_ln_b': (0.0, 0.1),
     'L3_conv_conv_b': (0.0, 0.1),
     'L3_conv_Ds': (1.0, 0.2),
     'L3_conv_ln_gamma': (1.0, 0.2),
     'L3_conv_ln_beta': (0.0, 0.1)}
    factors = {}
    for name, (base, spread) in spreads.items():
        noise = np.random.default_rng([zlib.crc32(name.encode()), seed]).standard_normal(out[name].shape)
        drawn = base * np.exp(spread * noise) if base else spread * noise
        out[name] = jnp.asarray(drawn.astype(out[name].dtype))
    for name, factor in factors.items():
        out[name] = (out[name] * factor).astype(out[name].dtype)
    return out
```

```python
from contextlib import ExitStack

import concourse.bass as bass
from concourse import mybir

F32 = mybir.dt.float32
BF16 = mybir.dt.bfloat16
ALU = mybir.AluOpType
ACT = mybir.ActivationFunctionType

NBATCH, SIDE, C = 4, 64, 192
IMG = SIDE * SIDE
T = NBATCH * IMG
CP, CT = 96, 2
NS = 16
DTR = 12
BLK = 512
NBLK = IMG // BLK
NCH = T // BLK
ROWS = BLK // SIDE
BCR = 2 * NS
DTP = 3 * BCR
XR = DTP + DTR
BIG = 3.0e38


class Phase:

    def __init__(self, nc, name):
        self.nc, self.name, self.sems = nc, name, []

    def __enter__(self):
        self.stack = ExitStack()
        return self

    def sb(self, name, shape, dt=F32):
        return self.stack.enter_context(self.nc.sbuf_tensor(f"{self.name}_{name}", shape, dt))

    def ps(self, name, shape, dt=F32):
        return self.stack.enter_context(self.nc.psum_tensor(f"{self.name}_{name}", shape, dt))

    def sem(self, name):
        s = self.nc.alloc_semaphore(f"{self.name}_{name}")
        self.sems.append(s)
        return s

    def __exit__(self, *exc):
        if exc[0] is None:
            self.nc.clear_and_free_semaphores(self.sems)
            self.nc.all_engine_barrier()
        self.stack.close()
        return False


def turns(t, parity):
    return 16 * (t // 2 + 1) if isinstance(t, int) else 8 * (t - parity) + 16


class Layer:

    def __init__(self, name, di):
        self.name, self.di = name, di
        self.p = 128 if di % 128 == 0 else 96
        self.nd = di // self.p


def load_selectors(nc, selectors, sel):
    with Phase(nc, "sel") as ph:
        wide = ph.sb("wide", [DTP, BCR, 128])
        loaded, cast = ph.sem("loaded"), ph.sem("cast")
        with nc.Block() as block:
            @block.sync
            def _(sp):
                sp.dma_start(wide[:], selectors).then_inc(loaded, 16)

            @block.vector
            def _(dve):
                dve.wait_ge(loaded, 16)
                nc.vector.tensor_copy(sel[:], wide[:]).then_inc(cast, 1)
                dve.wait_ge(cast, 1)


def group_norm_stats(nc, tag, x, group_mean, gn_scale, gn_shift):
    nt = CT * NBATCH
    with Phase(nc, f"{tag}_gn") as ph:
        img = ph.sb("img", [CP, 2, IMG])
        stats = ph.sb("stats", [CP, nt, NBLK, 6])
        mv = ph.sb("mv", [CP, nt, 2])
        dev = ph.sb("dev", [CP, nt])
        gmat = ph.sb("gmat", [CP, CP])
        gmean = ph.sb("gmean", [CP, nt])
        var = ph.sb("var", [CP, nt])
        std = ph.sb("std", [CP, nt])
        eps = ph.sb("eps", [CP, 1])
        mean_ps = ph.ps("mean_ps", [CP, BLK])
        var_ps = ph.ps("var_ps", [CP, BLK])
        gmat_loaded, img_used = ph.sem("gmat_loaded"), ph.sem("img_used")
        img_loaded = [ph.sem("img_loaded0"), ph.sem("img_loaded1")]
        stats_done, mv_done, step, mean_done, var_done, std_done = (
            ph.sem(s) for s in ("stats_done", "mv_done", "step", "mean_done", "var_done", "std_done"))
        with nc.Block() as block:
            @block.sync
            def _(sp):
                sp.dma_start(gmat[:], group_mean).then_inc(gmat_loaded, 16)
                for i in range(nt):
                    k, b = divmod(i, NBATCH)
                    if i >= 2:
                        sp.wait_ge(img_used, i - 1)
                    sp.dma_start(img[:, i % 2], x[k * CP:(k + 1) * CP, b * IMG:(b + 1) * IMG]
                                 ).then_inc(img_loaded[i % 2], 16)

            @block.vector
            def _(dve):
                dve.memset(eps[:], 1e-5)
                for i in range(nt):
                    dve.wait_ge(img_loaded[i % 2], 16 * (i // 2 + 1))
                    for j in range(NBLK):
                        last = nc.vector.bn_stats(stats[:, i, j], img[:, i % 2, j * BLK:(j + 1) * BLK])
                    last.then_inc(img_used, 1)
                dve.wait_ge(img_used, nt)
                for i in range(nt):
                    last = nc.vector.bn_aggr(mv[:, i], stats[:, i].rearrange("p a b -> p (a b)"))
                last.then_inc(mv_done, 1)
                dve.wait_ge(mean_done, 1)
                nc.vector.tensor_copy(gmean[:], mean_ps[:, 0:nt]).then_inc(step, 1)
                dve.wait_ge(step, 1)
                nc.vector.tensor_tensor(dev[:], mv[:, :, 0], gmean[:], ALU.subtract).then_inc(step, 1)
                dve.wait_ge(step, 2)
                nc.vector.tensor_tensor(dev[:], dev[:], dev[:], ALU.mult).then_inc(step, 1)
                dve.wait_ge(step, 3)
                nc.vector.tensor_tensor(var[:], dev[:], mv[:, :, 1], ALU.add).then_inc(step, 1)
                dve.wait_ge(std_done, 1)
                nc.vector.reciprocal(gn_scale[:], std[:]).then_inc(step, 1)
                dve.wait_ge(step, 5)
                nc.vector.scalar_tensor_tensor(out=gn_shift[:], in0=gmean[:], scalar=-1.0, in1=gn_scale[:],
                                               op0=ALU.mult, op1=ALU.mult)

            @block.tensor
            def _(pe):
                pe.wait_ge(gmat_loaded, 16)
                pe.wait_ge(mv_done, 1)
                nc.tensor.matmul(mean_ps[:, 0:nt], gmat[:], mv[:, :, 0], start=True, stop=True
                                 ).then_inc(mean_done, 1)
                pe.wait_ge(step, 4)
                nc.tensor.matmul(var_ps[:, 0:nt], gmat[:], var[:], start=True, stop=True).then_inc(var_done, 1)

            @block.scalar
            def _(act):
                act.wait_ge(var_done, 1)
                nc.scalar.activation(std[:], var_ps[:, 0:nt], ACT.Sqrt, bias=eps[:, 0:1]).then_inc(std_done, 1)


def project(nc, L, x, streams, conv2d, snake, gn_scale, gn_shift, z_out):
    P, nd = L.p, L.nd
    nk = len(streams)
    per_b = nk * nd
    nb = 2 if per_b % 2 == 0 else 3
    lead = 1 if conv2d else 3
    PW = SIDE + 2 * lead
    PH = SIDE + 2 if conv2d else SIDE
    taps = 9 if conv2d else 4
    half = SIDE // 2
    vertical_input = not conv2d
    with Phase(nc, f"{L.name}_proj") as ph:
        xraw = ph.sb("xraw", [CP, IMG])
        xn = ph.sb("xn", [CP, CT, IMG])
        xv = ph.sb("xv", [CP, CT, IMG]) if vertical_input else None
        w = ph.sb("w", [CP, nk, CT, 2 * L.di])
        cw = ph.sb("cw", [P, nk, nd, taps])
        cb = ph.sb("cb", [P, nk, nd])
        pad = [ph.sb(f"pad{i}", [P, PH, PW]) for i in range(nb)]
        conv = [ph.sb(f"conv{i}", [P, SIDE, SIDE]) for i in range(nb)]
        turned = ph.sb("turned", [P, SIDE, SIDE]) if conv2d else None
        gate = ph.sb("gate", [P, IMG])
        acc = ph.ps("acc", [128, NBLK, BLK])
        (w_loaded, xraw_loaded, xn_ready, xv_ready, mm_done, evacuated, pads_zero, conv_step, silu_done,
         turned_done, gate_done, gate_stored, uc_stored, ucv_stored) = (ph.sem(s) for s in (
             "w_loaded", "xraw_loaded", "xn_ready", "xv_ready", "mm_done", "evacuated", "pads_zero", "conv_step",
             "silu_done", "turned_done", "gate_done", "gate_stored", "uc_stored", "ucv_stored"))
        steps = 2 * taps
        n_w = 3 * nk
        prepare = (8, 14) if conv2d else (6, 7)

        def tiles():
            return [(k, j) for k in range(nk) for j in range(nd)]

        def batches(eng, body):
            body(0, True, False)
            with eng.Fori(1, NBATCH - 1) as b:
                body(b, False, False)
            body(NBATCH - 1, False, True)

        with nc.Block() as block:
            @block.sync
            def _(sp):
                for k, s in enumerate(streams):
                    sp.dma_start(w[:, k], s["w"].rearrange("(t p) n -> p t n", p=CP)).then_inc(w_loaded, 16)
                    sp.dma_start(cw[:, k], s["cw"]).then_inc(w_loaded, 16)
                    sp.dma_start(cb[:, k], s["cb"]).then_inc(w_loaded, 16)

                def store_uc(b, q):
                    k, j = tiles()[q]
                    s, tile = streams[k], per_b * b + q
                    rows = slice(j * P, (j + 1) * P)
                    buf = conv[q % nb]
                    img = bass.ds(b * IMG, IMG)
                    sp.wait_ge(silu_done, tile + 1)
                    src = turned if snake else buf
                    sp.dma_start(s["h"][rows, img], src[:].rearrange("p a b -> p (a b)")).then_inc(uc_stored, 16)
                    if "v" in s:
                        sp.wait_ge(turned_done, tile + 1)
                        sp.dma_start(s["v"][rows, img], turned[:].rearrange("p a b -> p (a b)")
                                     ).then_inc(ucv_stored, 16)

                def load_x(b, t):
                    if t or not isinstance(b, int) or b:
                        sp.wait_ge(xn_ready, b * CT + t)
                    sp.dma_start(xraw[:], x[t * CP:(t + 1) * CP, bass.ds(b * IMG, IMG)]
                                 ).then_inc(xraw_loaded, 16)

                load_x(0, 0)
                load_x(0, 1)

                def body(b, first, last):
                    if not last:
                        load_x(b + 1, 0)
                    for q, (k, j) in enumerate(tiles()):
                        if q or not first:
                            store_uc(b if q else b - 1, q - 1 if q else per_b - 1)
                        sp.wait_ge(gate_done, per_b * b + q + 1)
                        sp.dma_start(z_out[k][j * P:(j + 1) * P, bass.ds(b * IMG, IMG)], gate[:]
                                     ).then_inc(gate_stored, 16)
                    if not last:
                        load_x(b + 1, 1)

                batches(sp, body)
                store_uc(NBATCH - 1, per_b - 1)
                sp.wait_ge(gate_stored, 16 * per_b * NBATCH)
                sp.wait_ge(uc_stored, 16 * per_b * NBATCH)
                if conv2d and not snake:
                    sp.wait_ge(ucv_stored, 16 * per_b * NBATCH)

            @block.tensor
            def _(pe):
                pe.wait_ge(w_loaded, 16 * n_w)

                def body(b, first, last_):
                    pe.wait_ge(xn_ready, CT * (b + 1))
                    for q, (k, j) in enumerate(tiles()):
                        src = xn
                        if streams[k].get("vertical"):
                            src = xv
                            pe.wait_ge(xv_ready, CT * (b + 1))
                        for part in range(2):
                            col = part * L.di + j * P
                            for i in range(NBLK):
                                n = (per_b * b + q) * 2 * NBLK + part * NBLK + i
                                if not (first and q == 0 and part == 0):
                                    pe.wait_ge(evacuated, n + 1 - NBLK)
                                for t in range(CT):
                                    last = nc.tensor.matmul(acc[0:P, i], w[:, k, t, col:col + P],
                                                            src[:, t, i * BLK:(i + 1) * BLK],
                                                            start=(t == 0), stop=(t == CT - 1))
                                last.then_inc(mm_done, 1)

                batches(pe, body)

            @block.scalar
            def _(act):
                def silu_conv(b, q):
                    k, j = tiles()[q]
                    tile = per_b * b + q
                    buf = conv[q % nb]
                    act.wait_ge(conv_step, steps * (tile + 1))
                    bias = cb[:, k, j:j + 1]
                    if snake:
                        if q or not isinstance(b, int) or b:
                            act.wait_ge(uc_stored, 16 * tile)
                        nc.scalar.activation(turned[:, 0::2, :], buf[:, 0::2, :], ACT.Silu, bias=bias)
                        nc.scalar.activation(turned[:, 1::2, :], buf[:, 1::2, ::-1], ACT.Silu, bias=bias
                                             ).then_inc(silu_done, 1)
                    else:
                        nc.scalar.activation(buf[:], buf[:], ACT.Silu, bias=bias).then_inc(silu_done, 1)
                        if conv2d:
                            act.wait_ge(silu_done, tile + 1)
                            if q or not isinstance(b, int) or b:
                                act.wait_ge(ucv_stored, 16 * tile)
                            nc.scalar.activation(turned[:], buf[:].rearrange("p r c -> p c r"), ACT.Copy
                                                 ).then_inc(turned_done, 1)

                act.wait_ge(pads_zero, 1)
                act.wait_ge(w_loaded, 16 * n_w)

                def turn_x(b, first):
                    if not first:
                        act.wait_ge(mm_done, per_b * b * 2 * NBLK)
                    for t in range(CT):
                        act.wait_ge(xn_ready, CT * b + t + 1)
                        nc.scalar.activation(xv[:, t].rearrange("p (c r) -> p c r", c=SIDE),
                                             xn[:, t].rearrange("p (r c) -> p c r", c=SIDE), ACT.Copy
                                             ).then_inc(xv_ready, 1)

                def body(b, first, last):
                    for q, (k, j) in enumerate(tiles()):
                        if vertical_input and q == nd:
                            turn_x(b, first)
                        n0 = (per_b * b + q) * 2 * NBLK
                        if not (first and q < nb):
                            act.wait_ge(conv_step, steps * (per_b * b + q - nb + 1))
                        for i in range(NBLK):
                            act.wait_ge(mm_done, n0 + i + 1)
                            r0 = (1 if conv2d else 0) + i * ROWS
                            nc.scalar.activation(pad[q % nb][:, r0:r0 + ROWS, lead:lead + SIDE],
                                                 acc[0:P, i].rearrange("p (a b) -> p a b", b=SIDE),
                                                 ACT.Copy).then_inc(evacuated, 1)
                        if not (first and q == 0):
                            act.wait_ge(gate_stored, 16 * (per_b * b + q))
                        for i in range(NBLK):
                            act.wait_ge(mm_done, n0 + NBLK + i + 1)
                            nc.scalar.activation(gate[:, i * BLK:(i + 1) * BLK], acc[0:P, i], ACT.Silu
                                                 ).then_inc(evacuated, 1)
                        act.wait_ge(evacuated, n0 + 2 * NBLK)
                        act.sem_inc(gate_done, 1)
                        if q or not first:
                            silu_conv(b if q else b - 1, q - 1 if q else per_b - 1)

                batches(act, body)
                silu_conv(NBATCH - 1, per_b - 1)

            @block.vector
            def _(dve):
                for p_ in pad:
                    last = dve.memset(p_[:], 0.0)
                last.then_inc(pads_zero, 1)
                dve.wait_ge(w_loaded, 16 * n_w)

                def normalise(b, t):
                    dve.wait_ge(xraw_loaded, 16 * (CT * b + t + 1))
                    if not isinstance(b, int) or b:
                        dve.wait_ge(mm_done, per_b * b * 2 * NBLK)
                        if vertical_input:
                            dve.wait_ge(xv_ready, CT * b)
                    col = bass.ds(t * NBATCH + b, 1)
                    nc.vector.tensor_scalar(xn[:, t], xraw[:], gn_scale[:, col], gn_shift[:, col],
                                            ALU.mult, ALU.add).then_inc(xn_ready, 1)

                normalise(0, 0)
                normalise(0, 1)

                def convolve(b, q, first, last):
                    k, j = tiles()[q]
                    tile = per_b * b + q
                    dve.wait_ge(evacuated, tile * 2 * NBLK + NBLK)
                    if not (first and q < nb):
                        dve.wait_ge(silu_done, tile - nb + 1)
                        if not snake:
                            dve.wait_ge(uc_stored, 16 * (tile - nb + 1))
                        if conv2d and not snake:
                            dve.wait_ge(turned_done, tile - nb + 1)
                    for i in range(steps):
                        tap, h = divmod(i, 2)
                        if conv2d:
                            r0, c0 = tap // 3 + h * half, tap % 3
                        else:
                            r0, c0 = h * half, (6 - tap if streams[k]["reverse"] else tap)
                        src = pad[q % nb][:, r0:r0 + half, c0:c0 + SIDE]
                        dst = conv[q % nb][:, h * half:(h + 1) * half, :]
                        wt = cw[:, k, j, tap:tap + 1]
                        if tap == 0:
                            nc.vector.tensor_scalar(dst, src, wt, None, ALU.mult).then_inc(conv_step, 1)
                        else:
                            dve.wait_ge(conv_step, steps * tile + i - 1)
                            nc.vector.scalar_tensor_tensor(out=dst, in0=src, scalar=wt, in1=dst,
                                                           op0=ALU.mult, op1=ALU.add).then_inc(conv_step, 1)
                        if q == per_b - 1 and not last and i in prepare:
                            normalise(b + 1, prepare.index(i))

                def body(b, first, last):
                    for q in range(per_b):
                        convolve(b, q, first, last)

                batches(dve, body)


def scan_pass(nc, tag, L, uc, y, y_add, par, skips, reverse, segmented, ident, sel, keep,
              bias_twice=False):
    P, nd = L.p, L.nd
    XPROJ, SUB1, SUB2, DELTA = 3, 4, 5, 6
    COPY_Y, HI, MID, LO, BIAS = 4, 6, 7, 8, 9
    FINISH, SOFT = 1, 13
    TIMES_U = 13
    G = 8
    NDA, NPR, NCS, NBC = 4, 4, 4, 2
    W = BLK if segmented else BLK + 1
    d0 = 1 if (not segmented and not reverse) else 0
    cin = 0 if not reverse else BLK
    cout = BLK if not reverse else 0
    with Phase(nc, tag) as ph:
        xw = ph.sb("xw", [P, nd, XR])
        dtw = ph.sb("dtw", [128, L.di])
        dtb = ph.sb("dtb", [P, nd])
        alog = ph.sb("alog", [P, nd, NS])
        a_neg = ph.sb("a_neg", [P, nd, NS])
        dskip = ph.sb("dskip", [P, max(1, len(skips)), nd])
        eye = ph.sb("eye", [P, P])
        minus_eye = ph.sb("minus_eye", [DTP, DTP], BF16)
        bounds = ph.sb("bounds", [P, 2, NCH])
        u = [ph.sb(f"u{i}", [P, nd, BLK]) for i in range(2)]
        delta = [ph.sb(f"delta{i}", [P, nd, BLK]) for i in range(2)]
        du = [ph.sb(f"du{i}", [P, nd, BLK]) for i in range(2)]
        dts = ph.sb("dts", [128, BLK])
        parts = [ph.sb(f"parts{i}", [DTP, BLK], BF16) for i in range(2)]
        pre = ph.sb("pre", [P, nd, BLK])
        soft = ph.sb("soft", [P, nd, BLK])
        dA = ph.sb("dA", [P, NDA, nd, W])
        S = ph.sb("S", [P, G, nd, W])
        carry = ph.sb("carry", [P, NS, nd])
        prod = ph.sb("prod", [P, NPR, nd, BLK])
        Cs = ph.sb("Cs", [P, NCS, BLK])
        yo = ph.sb("yo", [P, nd, BLK])
        yp = ph.sb("yp", [P, nd, BLK]) if y_add else None
        y_ps = ph.ps("y_ps", [P, nd, BLK])
        b_ps = ph.ps("b_ps", [P, NBC, BLK])
        c_ps = ph.ps("c_ps", [P, NBC, BLK])
        m_ps = ph.ps("m_ps", [128, BLK])
        (w_loaded, a_exp, a_ready, consts_set, xproj_done, dts_ready, hi_done, sub1_done, mid_done,
         sub2_done, parts_ready, low_done, pre_ready, exp_done, log_done, delta_ready, du_ready,
         b_spread, c_spread, dbu_done, da_ready, scanned, c_copied, prod_ready, prod_used, carry_in, carry_out,
         y_ready, y_stored, yp_loaded, y_read) = (ph.sem(s) for s in (
             "w_loaded", "a_exp", "a_ready", "consts_set", "xproj_done", "dts_ready", "hi_done",
             "sub1_done", "mid_done", "sub2_done", "parts_ready", "low_done", "pre_ready", 
             "exp_done", "log_done", "delta_ready", "du_ready", "b_spread", "c_spread", "dbu_done", "da_ready",
             "scanned", "c_copied", "prod_ready", "prod_used", "carry_in", "carry_out", "y_ready", "y_stored",
             "yp_loaded", "y_read"))
        u_loaded = [ph.sem("u_loaded0"), ph.sem("u_loaded1")]

        def tokens(c):
            return bass.ds(c * -BLK + (NCH - 1) * BLK if reverse else c * BLK, BLK)

        def chunks(eng, body):
            body(0, 0, True, False)
            with eng.Fori(0, (NCH - 2) // 2) as i:
                body(2 * i + 1, 1, False, False)
                body(2 * i + 2, 0, False, False)
            body(NCH - 1, 1, False, True)

        def tiles(ap):
            return ap.rearrange("(k p) t -> p k t", p=P)

        def flat(ap):
            v = ap.rearrange("p d w -> p (d w)")
            return v[:, ::-1] if reverse else v

        def wide(ap):
            return ap.unsqueeze(1).to_broadcast([P, nd, BLK])

        loads = [(xw[:, :, i * BCR:(i + 1) * BCR], par["xw"][:, DTR:].rearrange("(k p) n -> p k n", p=P))
                 for i in range(3)]
        loads += [(xw[:, :, DTP:XR], par["xw"][:, 0:DTR].rearrange("(k p) n -> p k n", p=P)),
                  (dtw[DTP:XR, :], par["dtw"]), (dtb[:], par["dtb"]), (alog[:], par["alog"]),
                  (eye[:], ident[0:P, 0:P]), 
                  (bounds[:], keep[0:P])]
        loads += [(dskip[:, i], src) for i, src in enumerate(skips)]
        n_w = 16 * len(loads)

        with nc.Block() as block:
            @block.sync
            def _(sp):
                for dst, src in loads:
                    sp.dma_start(dst, src).then_inc(w_loaded, 16)
                sp.dma_start(u[0][:], tiles(uc)[:, :, tokens(0)]).then_inc(u_loaded[0], 16)
                if y_add:
                    sp.dma_start(yp[:], tiles(y_add)[:, :, tokens(0)]).then_inc(yp_loaded, 16)

                def finish(c):
                    if y_add:
                        sp.wait_ge(y_ready, c + 1)
                    else:
                        sp.wait_ge(y_read, nd * (c + 1))
                    sp.dma_start(tiles(y)[:, :, tokens(c)], yo[:]).then_inc(y_stored, 16)

                def body(c, par_, first, last):
                    if not first:
                        finish(c - 1)
                        if y_add:
                            sp.dma_start(yp[:], tiles(y_add)[:, :, tokens(c)]).then_inc(yp_loaded, 16)
                    if not last:
                        sp.dma_start(u[1 - par_][:], tiles(uc)[:, :, tokens(c + 1)]
                                     ).then_inc(u_loaded[1 - par_], 16)

                chunks(sp, body)
                finish(NCH - 1)
                sp.wait_ge(y_stored, 16 * NCH)

            @block.tensor
            def _(pe):
                pe.wait_ge(w_loaded, n_w)

                def xproj(c, q):
                    pe.wait_ge(u_loaded[q], turns(c, q))
                    if not isinstance(c, int) or c:
                        pe.wait_ge(pre_ready, nd * c)
                    for d in range(nd):
                        last = nc.tensor.matmul(m_ps[0:XR, :], xw[:, d], u[q][:, d], start=(d == 0),
                                                stop=(d == nd - 1))
                    last.then_inc(xproj_done, 1)

                def subtract(c, q, part_done, sub_done):
                    pe.wait_ge(part_done, c + 1)
                    nc.tensor.matmul(m_ps[0:DTP, :], minus_eye[:], parts[q][:], start=False, stop=True,
                                     skip_group_check=True).then_inc(sub_done, 1)

                def delta_mm(c, d):
                    pe.wait_ge(dts_ready, c + 1)
                    if d == 0:
                        pe.wait_ge(parts_ready, c + 1)
                    else:
                        pe.wait_ge(pre_ready, nd * c + d)
                    nc.tensor.matmul(m_ps[0:P, :], dtw[DTP:XR, d * P:(d + 1) * P], dts[DTP:XR, :],
                                     start=True, stop=True).then_inc(low_done, 1)

                def spread(c, n, q, early):
                    if n == 0:
                        pe.wait_ge(parts_ready, c + 1)
                    if not early:
                        pe.wait_ge(dbu_done, NS * c + n + 1 - NBC)
                    nc.tensor.matmul(b_ps[:, n % NBC], sel[:, n, 0:P], parts[q][:], start=True, stop=True
                                     ).then_inc(b_spread, 1)
                    if not early:
                        pe.wait_ge(c_copied, NS * c + n + 1 - NBC)
                    nc.tensor.matmul(c_ps[:, n % NBC], sel[:, NS + n, 0:P], parts[q][:], start=True, stop=True
                                     ).then_inc(c_spread, 1)

                LEAD = 4
                xproj(0, 0)
                pe.wait_ge(consts_set, 1)
                subtract(0, 0, hi_done, sub1_done)
                subtract(0, 0, mid_done, sub2_done)
                for d in range(nd):
                    delta_mm(0, d)
                for n in range(LEAD):
                    spread(0, n, 0, n < NBC)

                def body(c, q, first, last):
                    for n in range(NS):
                        if n + LEAD < NS:
                            spread(c, n + LEAD, q, False)
                        elif not last:
                            spread(c + 1, n + LEAD - NS, 1 - q, False)
                        if not last:
                            if n == XPROJ:
                                xproj(c + 1, 1 - q)
                            if n == SUB1:
                                subtract(c + 1, 1 - q, hi_done, sub1_done)
                            if n == SUB2:
                                subtract(c + 1, 1 - q, mid_done, sub2_done)
                            if DELTA <= n < DELTA + nd:
                                delta_mm(c + 1, n - DELTA)
                        pe.wait_ge(prod_ready, NS * c + n + 1)
                        for d in range(nd):
                            if n == 0 and not first:
                                pe.wait_ge(y_read, nd * (c - 1) + d + 1)
                            mm = nc.tensor.matmul(y_ps[:, d], eye[:], prod[:, n % NPR, d], start=(n == 0),
                                                  stop=(n == NS - 1))
                        mm.then_inc(prod_used, 1)

                chunks(pe, body)

            @block.scalar
            def _(act):
                nc.scalar.preload_act_table_set("natural_log_exp_and_others")
                act.wait_ge(w_loaded, n_w)
                nc.scalar.activation(a_neg[:], alog[:], ACT.Exp).then_inc(a_exp, 1)

                def split_hi(c, q):
                    act.wait_ge(xproj_done, c + 1)
                    if not isinstance(c, int) or c:
                        act.wait_ge(low_done, nd * c)
                        if not isinstance(c, int) or c >= 2:
                            act.wait_ge(b_spread, NS * (c - 1))
                            act.wait_ge(c_spread, NS * (c - 1))
                    nc.scalar.activation(dts[DTP:XR, :], m_ps[DTP:XR, :], ACT.Copy).then_inc(dts_ready, 1)
                    nc.scalar.activation(parts[q][:], m_ps[0:DTP, :], ACT.Copy).then_inc(hi_done, 1)

                def split_mid(c, q):
                    act.wait_ge(sub1_done, c + 1)
                    nc.scalar.activation(parts[q][0:2 * BCR, :], m_ps[0:2 * BCR, :], ACT.Copy).then_inc(mid_done, 1)

                def split_lo(c, q):
                    act.wait_ge(sub2_done, c + 1)
                    nc.scalar.activation(parts[q][0:BCR, :], m_ps[0:BCR, :], ACT.Copy).then_inc(parts_ready, 1)

                def add_bias(c, d):
                    act.wait_ge(low_done, nd * c + d + 1)
                    if d == 0 and (not isinstance(c, int) or c):
                        act.wait_ge(delta_ready, c)
                    nc.scalar.activation(pre[:, d], m_ps[0:P, :], ACT.Identity, bias=dtb[:, d:d + 1])
                    nc.scalar.activation(soft[:, d], m_ps[0:P, :], ACT.Abs, bias=dtb[:, d:d + 1]
                                         ).then_inc(pre_ready, 1)

                def soft_exp(c):
                    act.wait_ge(pre_ready, nd * (c + 1))
                    nc.scalar.activation(soft[:], soft[:], ACT.Exp, scale=-1.0).then_inc(exp_done, 1)

                def soft_log(c):
                    act.wait_ge(exp_done, c + 1)
                    nc.scalar.activation(soft[:], soft[:], ACT.Ln, bias=1.0).then_inc(log_done, 1)

                act.wait_ge(a_ready, 1)
                split_hi(0, 0)
                split_mid(0, 0)
                split_lo(0, 0)
                for d in range(nd):
                    add_bias(0, d)
                soft_exp(0)
                soft_log(0)
                act.wait_ge(consts_set, 1)

                def copy_y(c):
                    act.wait_ge(prod_used, NS * (c + 1))
                    if not isinstance(c, int) or c:
                        act.wait_ge(y_stored, 16 * c)
                    for d in range(nd):
                        nc.scalar.activation(yo[:, d], y_ps[:, d], ACT.Copy).then_inc(y_read, 1)

                def body(c, q, first, last):
                    for n in range(NS):
                        if n == 0:
                            act.wait_ge(delta_ready, c + 1)
                        if not (first and n < NDA):
                            act.wait_ge(scanned, NS * c + n + 1 - NDA)
                        for d in range(nd):
                            dst, src = dA[:, n % NDA, d], delta[q][:, d]
                            if segmented:
                                keep_ = slice(0, SIDE - 1) if reverse else slice(1, SIDE)
                                dst = dst.rearrange("p (s l) -> p s l", l=SIDE)[:, :, keep_]
                                src = src.rearrange("p (s l) -> p s l", l=SIDE)[:, :, keep_]
                            else:
                                dst = dst[:, d0:d0 + BLK]
                            e = nc.scalar.activation(dst, src, ACT.Exp, scale=a_neg[:, d, n:n + 1])
                        e.then_inc(da_ready, 1)
                        act.wait_ge(c_spread, NS * c + n + 1)
                        if not (first and n < NCS):
                            act.wait_ge(prod_ready, NS * c + n + 1 - NCS)
                        nc.scalar.activation(Cs[:, n % NCS], c_ps[:, n % NBC], ACT.Copy).then_inc(c_copied, 1)
                        if n == COPY_Y and not first and not skips:
                            copy_y(c - 1)
                        if not last:
                            if n == HI:
                                split_hi(c + 1, 1 - q)
                            if n == MID:
                                split_mid(c + 1, 1 - q)
                            if n == LO:
                                split_lo(c + 1, 1 - q)
                            if BIAS <= n < BIAS + nd:
                                add_bias(c + 1, n - BIAS)
                            if n == BIAS + nd:
                                soft_exp(c + 1)
                            if n == BIAS + nd + 1:
                                soft_log(c + 1)

                chunks(act, body)
                if not skips:
                    copy_y(NCH - 1)

            @block.vector
            def _(dve):
                for b in range(NDA):
                    if segmented:
                        v = dA[:, b].rearrange("p d (s l) -> p (d s) l", l=SIDE)
                        z = v[:, :, SIDE - 1] if reverse else v[:, :, 0]
                    else:
                        z = dA[:, b, :, cin]
                    dve.memset(z, 0.0)
                dve.memset(carry[:], 0.0)
                dve.wait_ge(w_loaded, n_w)
                if len(skips) == 2:
                    nc.vector.tensor_tensor(dskip[:, 0], dskip[:, 0], dskip[:, 1], ALU.add)
                nc.vector.tensor_scalar(minus_eye[:], eye[0:DTP, 0:DTP], -1.0, None, ALU.mult
                                        ).then_inc(consts_set, 1)
                if bias_twice:
                    nc.vector.tensor_scalar(dtb[:], dtb[:], 2.0, None, ALU.mult)
                dve.wait_ge(a_exp, 1)
                nc.vector.tensor_scalar(a_neg[:], a_neg[:], -1.0, None, ALU.mult).then_inc(a_ready, 1)

                def soft_plus(c, q):
                    dve.wait_ge(log_done, c + 1)
                    nc.vector.scalar_tensor_tensor(out=delta[q][:], in0=pre[:], scalar=0.0, in1=soft[:],
                                                   op0=ALU.max, op1=ALU.add).then_inc(delta_ready, 1)

                soft_plus(0, 0)

                def finish(c, q):
                    dve.wait_ge(prod_used, NS * (c + 1))
                    if not isinstance(c, int) or c:
                        dve.wait_ge(y_stored, 16 * c)
                    for d in range(nd):
                        e = nc.vector.scalar_tensor_tensor(out=yo[:, d], in0=u[q][:, d],
                                                           scalar=dskip[:, 0, d:d + 1], in1=y_ps[:, d],
                                                           op0=ALU.mult, op1=ALU.add).then_inc(y_read, 1)
                    if y_add:
                        dve.wait_ge(yp_loaded, 16 * (c + 1))
                        dve.wait_ge(y_read, nd * (c + 1))
                        nc.vector.tensor_tensor(yo[:], yo[:], yp[:], ALU.add).then_inc(y_ready, 1)

                def body(c, q, first, last):
                    def dbu(n):
                        if n == 0:
                            dve.wait_ge(du_ready, c + 1)
                        if not (first and n < G):
                            dve.wait_ge(prod_ready, NS * c + n + 1 - G)
                        dve.wait_ge(b_spread, NS * c + n + 1)
                        nc.vector.tensor_tensor(S[:, n % G, :, d0:d0 + BLK], du[q][:],
                                                wide(b_ps[:, n % NBC]), ALU.mult).then_inc(dbu_done, 1)

                    for g in range(NS // G):
                        gs = slice(g * G, (g + 1) * G)
                        if not segmented:
                            if not (first and g == 0):
                                dve.wait_ge(carry_out, (NS // G) * c + g)
                            nc.vector.tensor_scalar(S[:, :, :, cin], carry[:, gs, :],
                                                    bounds[:, 0, bass.ds(c, 1)], bounds[:, 1, bass.ds(c, 1)],
                                                    ALU.max, ALU.min).then_inc(carry_in, 1)
                        dbu(g * G)
                        for j in range(G):
                            n = g * G + j
                            if j + 1 < G:
                                dbu(n + 1)
                            if j == 0 and not segmented:
                                dve.wait_ge(carry_in, (NS // G) * c + g + 1)
                            dve.wait_ge(da_ready, NS * c + n + 1)
                            dve.wait_ge(dbu_done, NS * c + n + 1)
                            nc.vector.tensor_tensor_scan(flat(S[:, n % G]), flat(dA[:, n % NDA]),
                                                         flat(S[:, n % G]), 0.0, ALU.mult, ALU.add
                                                         ).then_inc(scanned, 1)
                            if n == FINISH and not first and skips:
                                finish(c - 1, 1 - q)
                            if not last:
                                if n == SOFT:
                                    soft_plus(c + 1, 1 - q)
                        if not segmented:
                            dve.wait_ge(scanned, NS * c + (g + 1) * G)
                            nc.vector.tensor_copy(carry[:, gs, :], S[:, :, :, cout]).then_inc(carry_out, 1)

                dve.wait_ge(w_loaded, n_w)
                dve.wait_ge(consts_set, 1)
                chunks(dve, body)
                if skips:
                    finish(NCH - 1, 1)

            @block.gpsimd
            def _(pool):
                def times_u(c, q):
                    pool.wait_ge(delta_ready, c + 1)
                    nc.gpsimd.tensor_tensor(du[q][:], delta[q][:], u[q][:], ALU.mult).then_inc(du_ready, 1)

                times_u(0, 0)

                def body(c, q, first, last):
                    for n in range(NS):
                        pool.wait_ge(scanned, NS * c + n + 1)
                        pool.wait_ge(c_copied, NS * c + n + 1)
                        if not (first and n < NPR):
                            pool.wait_ge(prod_used, NS * c + n + 1 - NPR)
                        nc.gpsimd.tensor_tensor(prod[:, n % NPR], S[:, n % G, :, d0:d0 + BLK],
                                                wide(Cs[:, n % NCS]), ALU.mult).then_inc(prod_ready, 1)
                        if n == TIMES_U and not last:
                            times_u(c + 1, 1 - q)

                chunks(pool, body)


def merge_norm(nc, L, x, x_out, yh, yv, z, par, ident_mean):
    P, nd = L.p, L.nd
    snake = not yv
    NY = 4
    with Phase(nc, f"{L.name}_merge") as ph:
        ow = ph.sb("ow", [P, nd, C])
        gam = ph.sb("gam", [P, nd])
        bet = ph.sb("bet", [P, nd])
        eps = ph.sb("eps", [P, 1])
        ones = ph.sb("ones", [P, P])
        yimg = [ph.sb(f"yimg{i}", [P, nd, IMG]) for i in range(2)] if yv else None
        yb = [ph.sb(f"yb{i}", [P, nd, BLK]) for i in range(2)]
        ys = [ph.sb(f"ys{i}", [P, nd, BLK]) for i in range(NY)]
        zb = [ph.sb(f"zb{i}", [P, nd, BLK]) for i in range(2)]
        xb = [ph.sb(f"xb{i}", [CP, CT, BLK]) for i in range(2)]
        sq = ph.sb("sq", [P, nd, BLK])
        std = ph.sb("std", [P, BLK])
        rstd = ph.sb("rstd", [P, BLK])
        mean_ps = ph.ps("mean_ps", [P, BLK])
        var_ps = ph.ps("var_ps", [P, BLK])
        out_ps = ph.ps("out_ps", [CP, CT, BLK])
        (w_loaded, summed, mean_done, centred, squared, var_done, std_done, rstd_done, scaled, affine,
         gated, out_done, x_ready) = (ph.sem(s) for s in (
             "w_loaded", "summed", "mean_done", "centred", "squared", "var_done", "std_done", "rstd_done",
             "scaled", "affine", "gated", "out_done", "x_ready"))
        yb_loaded, zb_loaded, xb_loaded, yimg_loaded, x_stored = (
            [ph.sem(f"{n}{i}") for i in range(2)]
            for n in ("yb_loaded", "zb_loaded", "xb_loaded", "yimg_loaded", "x_stored"))
        loads = [(ow[:], par["ow"].rearrange("(k p) n -> p k n", p=P)), (gam[:], par["g"]), (bet[:], par["b"]),
                 (ones[:], ident_mean[0:P, 0:P])]
        n_w = 16 * len(loads)
        DEPTH = 4

        def tiles(ap, p_):
            return ap.rearrange("(k p) t -> p k t", p=p_)

        def wide(ap):
            return ap.unsqueeze(1).to_broadcast([P, nd, BLK])

        def turns_of(eng, body):
            for b in range(NBATCH):
                for r in range(NY if b == 0 else 0):
                    body(r, r, b, r, [r >= s for s in range(DEPTH + 1)])
                n0 = NY if b == 0 else 0
                with eng.Fori(0, (NBLK - n0) // NY) as i:
                    for r in range(NY):
                        body(b * NBLK + n0 + r + NY * i, r, b, n0 + r + NY * i, [True] * (DEPTH + 1))
            for r in range(DEPTH):
                body(NCH + r, r, None, 0, [s > r for s in range(DEPTH + 1)])

        def early(t, n):
            return isinstance(t, int) and t < n

        with nc.Block() as block:
            @block.sync
            def _(sp):
                for dst, src in loads:
                    sp.dma_start(dst, src).then_inc(w_loaded, 16)

                def load_image(b):
                    if b >= 2:
                        sp.wait_ge(summed, NBLK * (b - 1))
                    sp.dma_start(yimg[b % 2][:], tiles(yv[0], P)[:, :, b * IMG:(b + 1) * IMG]
                                 ).then_inc(yimg_loaded[b % 2], 16)

                if yv:
                    load_image(0)

                def body(t, r, b, blk, live):
                    h = r % 2
                    if live[0]:
                        at = bass.ds(t * BLK, BLK)
                        if not early(t, 2):
                            sp.wait_ge(summed, t - 1)
                        sp.dma_start(yb[h][:], tiles(yh[0], P)[:, :, at]).then_inc(yb_loaded[h], 16)
                    if live[2]:
                        if not early(t - 2, 2):
                            sp.wait_ge(out_done, t - 3)
                        sp.dma_start(zb[h][:], tiles(z, P)[:, :, bass.ds((t - 2) * BLK, BLK)]
                                     ).then_inc(zb_loaded[h], 16)
                    if live[3]:
                        if not early(t - 3, 2):
                            sp.wait_ge(x_stored[1 - h], turns(t - 5, 1 - h))
                        sp.dma_start(xb[1 - h][:], tiles(x, CP)[:, :, bass.ds((t - 3) * BLK, BLK)]
                                     ).then_inc(xb_loaded[1 - h], 16)

                for b in range(NBATCH):
                    for r in range(NY if b == 0 else 0):
                        body(r, r, b, r, [r >= s for s in range(DEPTH + 1)])
                    if yv and b + 1 < NBATCH:
                        load_image(b + 1)
                    n0 = NY if b == 0 else 0
                    with sp.Fori(0, (NBLK - n0) // NY) as i:
                        for r in range(NY):
                            body(b * NBLK + n0 + r + NY * i, r, b, n0 + r + NY * i, [True] * (DEPTH + 1))
                for r in range(DEPTH):
                    body(NCH + r, r, None, 0, [s > r for s in range(DEPTH + 1)])

            @block.tensor
            def _(pe):
                pe.wait_ge(w_loaded, n_w)

                def body(t, r, b, blk, live):
                    if live[4]:
                        pe.wait_ge(gated, t - 3)
                        if not early(t - 4, 1):
                            pe.wait_ge(x_ready, t - 4)
                        for m in range(CT):
                            for d in range(nd):
                                mm = nc.tensor.matmul(out_ps[:, m], ow[:, d, m * CP:(m + 1) * CP],
                                                      zb[r % 2][:, d], start=(d == 0), stop=(d == nd - 1))
                        mm.then_inc(out_done, 1)
                    if live[0]:
                        pe.wait_ge(summed, t + 1)
                        if not early(t, 1):
                            pe.wait_ge(centred, t)
                        for d in range(nd):
                            mm = nc.tensor.matmul(mean_ps[:], ones[:], ys[r][:, d], start=(d == 0),
                                                  stop=(d == nd - 1))
                        mm.then_inc(mean_done, 1)
                    if live[1]:
                        pe.wait_ge(squared, t)
                        if not early(t - 1, 1):
                            pe.wait_ge(std_done, t - 1)
                        for d in range(nd):
                            mm = nc.tensor.matmul(var_ps[:], ones[:], sq[:, d], start=(d == 0), stop=(d == nd - 1))
                        mm.then_inc(var_done, 1)

                turns_of(pe, body)

            @block.vector
            def _(dve):
                dve.memset(eps[:], 1e-5)
                dve.wait_ge(w_loaded, n_w)

                def body(t, r, b, blk, live):
                    h = r % 2
                    if live[1]:
                        buf = ys[(r - 1) % NY]
                        dve.wait_ge(mean_done, t)
                        nc.vector.tensor_tensor(buf[:], buf[:], wide(mean_ps[:]), ALU.subtract
                                                ).then_inc(centred, 1)
                    if live[0]:
                        dve.wait_ge(yb_loaded[h], turns(t, h))
                        if not early(t, NY):
                            dve.wait_ge(gated, t - NY + 1)
                        if yv:
                            dve.wait_ge(yimg_loaded[b % 2], turns(b, b % 2))
                            for d in range(nd):
                                e = nc.vector.tensor_tensor(
                                    ys[r][:, d].rearrange("p (r c) -> p r c", c=SIDE),
                                    yb[h][:, d].rearrange("p (r c) -> p r c", c=SIDE),
                                    yimg[b % 2][:, d].rearrange("p (c r) -> p r c", r=SIDE)
                                    [:, bass.ds(blk * ROWS, ROWS), :], ALU.add)
                        else:
                            yr = yb[h][:].rearrange("p d (r c) -> p (d r) c", c=SIDE)
                            yw = ys[r][:].rearrange("p d (r c) -> p (d r) c", c=SIDE)
                            nc.vector.tensor_copy(yw[:, 0::2, :], yr[:, 0::2, :])
                            e = nc.vector.tensor_copy(yw[:, 1::2, :], yr[:, 1::2, ::-1])
                        e.then_inc(summed, 1)
                    if live[2]:
                        buf = ys[(r - 2) % NY]
                        if not early(t - 2, 1):
                            dve.wait_ge(scaled, t - 2)
                        dve.wait_ge(std_done, t - 1)
                        nc.vector.reciprocal(rstd[:], std[:]).then_inc(rstd_done, 1)
                        dve.wait_ge(rstd_done, t - 1)
                        nc.vector.tensor_tensor(buf[:], buf[:], wide(rstd[:]), ALU.mult).then_inc(scaled, 1)
                    if live[4]:
                        dve.wait_ge(out_done, t - 3)
                        dve.wait_ge(xb_loaded[h], turns(t - 4, h))
                        nc.vector.tensor_tensor(xb[h][:], out_ps[:], xb[h][:], ALU.add).then_inc(x_ready, 1)

                turns_of(dve, body)

            @block.scalar
            def _(act):
                act.wait_ge(w_loaded, n_w)

                def body(t, r, b, blk, live):
                    h = r % 2
                    if live[2]:
                        act.wait_ge(var_done, t - 1)
                        if not early(t - 2, 1):
                            act.wait_ge(rstd_done, t - 2)
                        nc.scalar.activation(std[:], var_ps[:], ACT.Sqrt, bias=eps[:, 0:1]).then_inc(std_done, 1)
                    if live[3]:
                        buf = ys[(r - 3) % NY]
                        act.wait_ge(scaled, t - 2)
                        for d in range(nd):
                            e = nc.scalar.activation(buf[:, d], buf[:, d], ACT.Identity,
                                                     scale=gam[:, d:d + 1], bias=bet[:, d:d + 1])
                        e.then_inc(affine, 1)
                    if live[1]:
                        act.wait_ge(centred, t)
                        if not early(t - 1, 1):
                            act.wait_ge(var_done, t - 1)
                        nc.scalar.activation(sq[:], ys[(r - 1) % NY][:], ACT.Square).then_inc(squared, 1)

                turns_of(act, body)

            @block.gpsimd
            def _(pool):
                def body(t, r, b, blk, live):
                    h = r % 2
                    if live[3]:
                        pool.wait_ge(zb_loaded[1 - h], turns(t - 3, 1 - h))
                        pool.wait_ge(affine, t - 2)
                        nc.gpsimd.tensor_tensor(zb[1 - h][:], zb[1 - h][:], ys[(r - 3) % NY][:], ALU.mult
                                                ).then_inc(gated, 1)
                    if live[4]:
                        pool.wait_ge(x_ready, t - 3)
                        pool.dma_start(tiles(x_out, CP)[:, :, bass.ds((t - 4) * BLK, BLK)], xb[h][:]
                                       ).then_inc(x_stored[h], 16)

                turns_of(pool, body)
                pool.wait_ge(x_stored[0], turns(NCH - 2, 0))
                pool.wait_ge(x_stored[1], turns(NCH - 1, 1))


def merge_four(nc, L, x, x_out, ys_dram, z_dram, out_w, fc_t, fc_b):
    P, nd = L.p, L.nd
    nk = 4
    quarter = [2, 3, 0, 1]
    with Phase(nc, f"{L.name}_merge") as ph:
        ow = ph.sb("ow", [CP, nk, CT, L.di])
        fc = ph.sb("fc", [CP, nk, CT, C])
        fw = ph.sb("fw", [P, nk, nd, C])
        fb = ph.sb("fb", [CP, CT])
        img = [ph.sb(f"img{i}", [CP, CT, IMG]) for i in range(2)]
        yb = [ph.sb(f"yb{i}", [P, nd, BLK]) for i in range(2)]
        zb = [ph.sb(f"zb{i}", [P, nd, BLK]) for i in range(2)]
        gb = [ph.sb(f"gb{i}", [P, nd, BLK]) for i in range(2)]
        fuse_ps = ph.ps("fuse_ps", [P, 2, BLK])
        out_ps = ph.ps("out_ps", [CP, 2, CT, BLK])
        (w_loaded, fused, fw_ready, gated, out_done, added, img_stored) = (ph.sem(s) for s in (
            "w_loaded", "fused", "fw_ready", "gated", "out_done", "added", "img_stored"))
        yb_loaded, zb_loaded, img_loaded = ([ph.sem(f"{n}_loaded{i}") for i in range(2)]
                                            for n in ("yb", "zb", "img"))
        n_w = 16 * (2 * nk + 1)

        def tiles(ap, p_):
            return ap.rearrange("(k p) t -> p k t", p=p_)

        def blocks(eng, body, start=None, end=None):
            for b in range(NBATCH):
                if start:
                    start(b)
                for k in range(nk):
                    t0 = (b * nk + k) * NBLK
                    body(t0, 0, b, k, 0, t0 == 0)
                    body(t0 + 1, 1, b, k, 1, t0 == 0)
                    with eng.Fori(0, (NBLK - 2) // 2) as i:
                        body(t0 + 2 + 2 * i, 0, b, k, 2 + 2 * i, False)
                        body(t0 + 3 + 2 * i, 1, b, k, 3 + 2 * i, False)
                if end:
                    end(b)

        with nc.Block() as block:
            @block.sync
            def _(sp):
                for k in range(nk):
                    sp.dma_start(ow[:, k], out_w[k].rearrange("(t p) n -> p t n", p=CP)).then_inc(w_loaded, 16)
                    sp.dma_start(fc[:, k], fc_t[quarter[k]].rearrange("(t p) n -> p t n", p=CP)
                                 ).then_inc(w_loaded, 16)
                sp.dma_start(fb[:], fc_b).then_inc(w_loaded, 16)

                def body(t, h, b, k, blk, first):
                    at = bass.ds(b * IMG + blk * BLK, BLK)
                    if not first:
                        sp.wait_ge(gated, t - 1)
                    sp.dma_start(yb[h][:], tiles(ys_dram[k], P)[:, :, at]).then_inc(yb_loaded[h], 16)
                    sp.dma_start(zb[h][:], tiles(z_dram[k], P)[:, :, at]).then_inc(zb_loaded[h], 16)

                blocks(sp, body)

            @block.gpsimd
            def _(pool):
                def load(b):
                    pool.dma_start(img[b % 2][:], tiles(x, CP)[:, :, b * IMG:(b + 1) * IMG]
                                   ).then_inc(img_loaded[b % 2], 16)

                def store(b):
                    pool.wait_ge(added, (b + 1) * nk * NBLK)
                    pool.dma_start(tiles(x_out, CP)[:, :, b * IMG:(b + 1) * IMG], img[b % 2][:]
                                   ).then_inc(img_stored, 16)

                load(0)
                for b in range(NBATCH):
                    if b + 1 < NBATCH:
                        if b:
                            pool.wait_ge(img_stored, 16 * b)
                        load(b + 1)
                    store(b)
                pool.wait_ge(img_stored, 16 * NBATCH)

            @block.tensor
            def _(pe):
                pe.wait_ge(w_loaded, n_w)
                for i in range(nk * nd):
                    k, d = divmod(i, nd)
                    if i >= 2:
                        pe.wait_ge(fw_ready, i - 1)
                    for t in range(CT):
                        mm = nc.tensor.matmul(fuse_ps[:, i % 2, 0:C], ow[:, k, t, d * P:(d + 1) * P], fc[:, k, t],
                                              start=(t == 0), stop=(t == CT - 1))
                    mm.then_inc(fused, 1)
                pe.wait_ge(fw_ready, nk * nd)

                def body(t, h, b, k, blk, first):
                    pe.wait_ge(gated, t + 1)
                    if not first:
                        pe.wait_ge(added, t - 1)
                    for m in range(CT):
                        for d in range(nd):
                            mm = nc.tensor.matmul(out_ps[:, h, m], fw[:, k, d, m * CP:(m + 1) * CP], gb[h][:, d],
                                                  start=(d == 0), stop=(d == nd - 1))
                    mm.then_inc(out_done, 1)

                blocks(pe, body)

            @block.scalar
            def _(act):
                for i in range(nk * nd):
                    k, d = divmod(i, nd)
                    act.wait_ge(fused, i + 1)
                    nc.scalar.activation(fw[:, k, d], fuse_ps[:, i % 2, 0:C], ACT.Copy).then_inc(fw_ready, 1)

            @block.vector
            def _(dve):
                dve.wait_ge(w_loaded, n_w)

                def gate(t, h, first):
                    dve.wait_ge(yb_loaded[h], turns(t, h))
                    dve.wait_ge(zb_loaded[h], turns(t, h))
                    if not first:
                        dve.wait_ge(out_done, t - 1)
                    nc.vector.tensor_tensor(gb[h][:], yb[h][:], zb[h][:], ALU.mult).then_inc(gated, 1)

                def add(t, h, b, k, blk):
                    dve.wait_ge(out_done, t + 1)
                    if k:
                        dve.wait_ge(added, (b * nk + k) * NBLK)
                    for m in range(CT):
                        if k < 2:
                            dst = img[b % 2][:, m, bass.ds(blk * BLK, BLK)]
                            src = out_ps[:, h, m]
                        else:
                            dst = img[b % 2][:, m].rearrange("p (r c) -> p c r", c=SIDE)
                            dst = dst[:, bass.ds(blk * ROWS, ROWS), :]
                            src = out_ps[:, h, m].rearrange("p (c r) -> p c r", r=SIDE)
                        if k == 0:
                            e = nc.vector.scalar_tensor_tensor(out=dst, in0=src, scalar=fb[:, m:m + 1], in1=dst,
                                                               op0=ALU.add, op1=ALU.add)
                        else:
                            e = nc.vector.tensor_tensor(dst, src, dst, ALU.add)
                    e.then_inc(added, 1)

                def body(t, h, b, k, blk, first):
                    gate(t, h, first)
                    if isinstance(blk, int) and blk == 0:
                        if t:
                            add(t - 1, 1 - h, *((b, k - 1) if k else (b - 1, nk - 1)), NBLK - 1)
                        if k == 0:
                            dve.wait_ge(img_loaded[b % 2], turns(b, b % 2))
                    else:
                        add(t - 1, 1 - h, b, k, blk - 1)

                blocks(dve, body)
                add(NBATCH * nk * NBLK - 1, 1, NBATCH - 1, nk - 1, NBLK - 1)


def build(nc, a, out):
    def scratch(name, rows):
        return nc.dram_tensor(name, [rows, T], F32, kind="Internal").ap()

    DI = 384
    L0, L1, L2, L3 = Layer("L0", DI), Layer("L1", DI), Layer("L2", C), Layer("L3", DI)
    uc = [scratch(f"uc{k}", DI) for k in range(4)]
    y = [scratch(f"y{k}", DI) for k in range(4)]
    z = [scratch(f"z{k}", DI) for k in range(4)]
    xs = [a["x"]] + [scratch(f"x{i}", C) for i in range(1, 4)] + [out]

    with ExitStack() as ctx:
        gn_scale = ctx.enter_context(nc.sbuf_tensor("gn_scale", [CP, CT * NBATCH], F32))
        gn_shift = ctx.enter_context(nc.sbuf_tensor("gn_shift", [CP, CT * NBATCH], F32))
        sel = ctx.enter_context(nc.sbuf_tensor("sel", [DTP, BCR, 128], BF16))
        load_selectors(nc, a["selectors"], sel)

        def norm(i):
            group_norm_stats(nc, f"L{i}", xs[i], a["group_mean"], gn_scale, gn_shift)

        def scan(L, k, src, dst, add, reverse, skips, segmented=False):
            par = {n: a[f"{L.name}_{n}"][k] for n in ("xw", "dtw", "dtb", "alog")}
            skips = [a[f"{L.name}_d"][i] for i in skips]
            scan_pass(nc, f"{L.name}_s{k}", L, src[0:L.di], dst[0:L.di], None if add is None else add[0:L.di],
                      par, skips, reverse, segmented, a["ident"], sel, a["keep"],
                      bias_twice=L.name == "L2")

        def merge(i, L, vertical):
            par = {n: a[f"{L.name}_{n}"] for n in ("ow", "g", "b")}
            merge_norm(nc, L, xs[i], xs[i + 1], [y[1 if vertical else 0][0:L.di]],
                       [y[3][0:L.di]] if vertical else [], z[0][0:L.di], par,
                       a["mean_384"] if L.di == DI else a["mean_192"])

        norm(0)
        project(nc, L0, xs[0], [dict(w=a["L0_w"][k], cw=a["L0_cw"][k], cb=a["L0_cb"][k], h=uc[k],
                                     vertical=k >= 2, reverse=k % 2 == 1) for k in range(4)],
                False, False, gn_scale, gn_shift, z)
        for k in range(4):
            scan(L0, k, uc[k], y[k], None, k % 2 == 1, [k], segmented=True)
        merge_four(nc, L0, xs[0], xs[1], y, z, a["L0_ow"], a["L0_fc"], a["L0_fb"])

        norm(1)
        project(nc, L1, xs[1], [dict(w=a["L1_w"], cw=a["L1_cw"], cb=a["L1_cb"], h=uc[0])],
                True, True, gn_scale, gn_shift, z)
        scan(L1, 0, uc[0], y[0], None, False, [0])
        merge(1, L1, False)

        for i, L, (hf, hr, vf, vr) in ((2, L2, (0, 1, 2, 3)), (3, L3, (0, 2, 1, 3))):
            norm(i)
            n = L.name
            project(nc, L, xs[i], [dict(w=a[f"{n}_w"], cw=a[f"{n}_cw"], cb=a[f"{n}_cb"], h=uc[0][0:L.di],
                                        v=uc[1][0:L.di])], True, False, gn_scale, gn_shift, z)
            scan(L, hf, uc[0], y[0], None, False, [])
            scan(L, hr, uc[0], y[1], y[0], True, [hf, hr])
            scan(L, vf, uc[1], y[2], None, False, [])
            scan(L, vr, uc[1], y[3], y[2], True, [vf, vr])
            merge(i, L, True)


def layouts(inputs):
    import numpy as np
    f = {k: np.asarray(v) for k, v in inputs.items()}

    def vec(v, lead, p):
        v = v.reshape(*lead, -1, p)
        return np.ascontiguousarray(np.swapaxes(v, -1, -2))

    def mat(v, lead, p, n):
        v = v.reshape(*lead, -1, p, n)
        return np.ascontiguousarray(np.swapaxes(v, -3, -2))

    def tr(v):
        return np.ascontiguousarray(np.swapaxes(v, -1, -2))

    a = {"x": np.ascontiguousarray(f["x"].transpose(3, 0, 1, 2).reshape(C, T))}
    q = "L0_conv_"
    a["L0_w"] = tr(f[q + "in_proj_w"])
    a["L0_cw"] = mat(f[q + "conv_w"], (4,), 128, 4)
    a["L0_cb"] = vec(f[q + "conv_b"], (4,), 128)
    a["L0_xw"] = tr(f[q + "x_proj_w"])
    a["L0_dtw"] = tr(f[q + "dt_proj_w"])
    a["L0_dtb"] = vec(f[q + "dt_proj_b"], (4,), 128)
    a["L0_alog"] = mat(f[q + "A_log"], (4,), 128, NS)
    a["L0_d"] = vec(f[q + "D_skip"], (4,), 128)
    a["L0_ow"] = np.ascontiguousarray(f[q + "out_proj_w"])
    a["L0_fc"] = tr(f[q + "fc_w"]).reshape(4, C, C)
    a["L0_fb"] = vec(f[q + "fc_b"], (), CP)
    q = "L1_conv_"
    a["L1_w"] = tr(f[q + "in_proj_w"])
    a["L1_cw"] = mat(f[q + "conv_w"], (), 128, 9)
    a["L1_cb"] = vec(f[q + "conv_b"], (), 128)
    a["L1_xw"] = tr(f[q + "x_proj_w"])[None]
    a["L1_dtw"] = tr(f[q + "dt_w"])[None]
    a["L1_dtb"] = vec(f[q + "dt_b"], (1,), 128)
    a["L1_alog"] = mat(f[q + "A_logs"], (1,), 128, NS)
    a["L1_d"] = vec(f[q + "Ds"], (1,), 128)
    a["L1_ow"] = tr(f[q + "out_proj_w"])
    a["L1_g"] = vec(f[q + "ln_w"], (), 128)
    a["L1_b"] = vec(f[q + "ln_b"], (), 128)
    q = "L2_conv_"
    a["L2_w"] = np.ascontiguousarray(f[q + "in_proj_w"])
    a["L2_cw"] = mat(f[q + "conv_w"], (), 96, 9)
    a["L2_cb"] = vec(f[q + "conv_b"], (), 96)
    a["L2_xw"] = np.ascontiguousarray(f[q + "x_proj_w"])
    a["L2_dtw"] = np.ascontiguousarray(f[q + "dt_w"])
    a["L2_dtb"] = vec(f[q + "dt_b"], (4,), 96)
    a["L2_alog"] = mat(f[q + "A_logs"], (4,), 96, NS)
    a["L2_d"] = vec(f[q + "Ds"], (4,), 96)
    a["L2_ow"] = np.ascontiguousarray(f[q + "out_w"])
    a["L2_g"] = vec(f[q + "ln_g"], (), 96)
    a["L2_b"] = vec(f[q + "ln_b"], (), 96)
    q = "L3_conv_"
    a["L3_w"] = tr(f[q + "in_proj_w"])
    a["L3_cw"] = mat(f[q + "conv_w"], (), 128, 9)
    a["L3_cb"] = vec(f[q + "conv_b"], (), 128)
    a["L3_xw"] = tr(f[q + "x_proj_weight"])
    a["L3_dtw"] = tr(f[q + "dt_projs_weight"])
    a["L3_dtb"] = vec(f[q + "dt_projs_bias"], (4,), 128)
    a["L3_alog"] = mat(f[q + "A_logs"], (4,), 128, NS)
    a["L3_d"] = vec(f[q + "Ds"], (4,), 128)
    a["L3_ow"] = tr(f[q + "out_proj_w"])
    a["L3_g"] = vec(f[q + "ln_gamma"], (), 128)
    a["L3_b"] = vec(f[q + "ln_beta"], (), 128)

    a["ident"] = np.eye(128, dtype=np.float32)
    a["mean_384"] = np.full((128, 128), 1 / 384, np.float32)
    a["mean_192"] = np.full((128, 128), 1 / 192, np.float32)
    a["group_mean"] = np.kron(np.eye(CP // 6), np.full((6, 6), 1 / 6)).astype(np.float32)
    rows = np.arange(DTP) % BCR
    sel = (rows[:, None, None] == np.arange(BCR)[None, :, None]) * np.ones((1, 1, 128))
    a["selectors"] = sel.astype(np.float32)
    bounds = np.full((128, 2, NCH), BIG, np.float32)
    bounds[:, 0] = -BIG
    bounds[:, :, ::NBLK] = 0.0
    a["keep"] = bounds
    return a


def kernel(**inputs):
    import numpy as _np
    import concourse.bacc as _bacc
    from concourse.bass_utils import run_bass_kernel_spmd as _run

    arrays = layouts(inputs)
    nc = _bacc.Bacc("TRN2", target_bir_lowering=False, num_devices=1)
    handles = {n: nc.dram_tensor(f"in_{n}", v.shape, mybir.dt.from_np(v.dtype), kind="ExternalInput").ap()
               for n, v in arrays.items()}
    out = nc.dram_tensor("out_0", [C, T], F32, kind="ExternalOutput").ap()
    build(nc, handles, out)
    r = _run(nc, [{f"in_{n}": v for n, v in arrays.items()}], core_ids=[0])
    got = r.results[0]["out_0"]
    return _np.ascontiguousarray(got.reshape(C, NBATCH, SIDE, SIDE).transpose(1, 2, 3, 0))
```
